# Optimizing a Trainium2 kernel written in Bass

```python
import numpy as np
import jax
import jax.numpy as jnp

def _softmax(x, axis=-1):
    return jax.nn.softmax(x, axis=axis)

def _gelu(x):
    return jax.nn.gelu(x, approximate=True)

def _silu(x):
    return jax.nn.silu(x)

def _sigmoid(x):
    return jax.nn.sigmoid(x)

def _layernorm(x, axis=-1, eps=1e-05):
    m = jnp.mean(x, axis=axis, keepdims=True)
    v = jnp.var(x, axis=axis, keepdims=True)
    return (x - m) / jnp.sqrt(v + eps)

def _scatter_add(tgt, idx, src, axis=0):
    return tgt.at[idx].add(src)

def _segment_sum(src, seg, n):
    return jax.ops.segment_sum(src, seg, n)
kernel_name = 'mk_flamingo_gated_d1_seqx_r8_b5b1f0'

def setup_inputs(seed: int=0):
    np.random.seed(seed)
    _w = jnp.asarray

    def _rec_inputs():
        import jax
        import jax.numpy as jnp
        _rk = jax.random.key(seed)
        x = -0.0003929 + 0.9999 * jax.random.normal(jax.random.fold_in(_rk, 1), (16, 128, 128), jnp.float32)
        _lenS = 128 - jax.random.randint(jax.random.fold_in(_rk, 7), (16,), 0, max(1, 128 // 4) + 1, jnp.int32)
        _lenS2 = 128 - jax.random.randint(jax.random.fold_in(_rk, 8), (16,), 0, max(1, 128 // 4) + 1, jnp.int32)
        _ctx_1024P = jax.random.normal(jax.random.fold_in(_rk, 11), (16, 16, 128), jnp.float32)
        _ctx_1024c = jax.random.dirichlet(jax.random.fold_in(_rk, 511), 0.3 * jnp.ones((16,), jnp.float32), (16, 128))
        _ctx_1024t = jnp.einsum('bsk,bkd->bsd', _ctx_1024c, _ctx_1024P)
        _ctx_1024t = _ctx_1024t * jax.lax.rsqrt(jnp.mean(jnp.square(_ctx_1024t)) + 1e-12) * 0.953939
        ctx_1024 = 2.81802e-05 + 1.00001 * (_ctx_1024t + 0.3 * jax.random.normal(jax.random.fold_in(_rk, 611), (16, 128, 128), jnp.float32))
        _g = jax.random.normal(jax.random.fold_in(_rk, 9001), (2, 1), jnp.float32)
        _g = jnp.sign(_g) * jnp.maximum(jnp.abs(_g), 1.0) + (_g == 0) * 1.0
        g_xattn = _g[0]
        g_ffn = _g[1]
        return (x, ctx_1024, g_xattn, g_ffn)
    x, ctx_1024, g_xattn, g_ffn = _rec_inputs()

    def _L0_xattn_setup():
        import jax, jax.numpy as jnp
        import numpy as np
        import math
        D_MODEL = 128
        NUM_HEADS = 16
        BATCH, SEQ = (4, 512)
        key = jax.random.key(seed)
        ks = jax.random.split(key, 7)
        s = 1.0 / math.sqrt(D_MODEL)
        return {'query': jax.random.normal(ks[0], (BATCH, SEQ, D_MODEL), jnp.float32), 'value': jax.random.normal(ks[1], (BATCH, SEQ, D_MODEL), jnp.float32), 'Wq': jax.random.normal(ks[2], (D_MODEL, D_MODEL), jnp.float32) * s, 'bq': jax.random.normal(ks[3], (D_MODEL,), jnp.float32) * s, 'qk_b': jnp.zeros((D_MODEL,), jnp.float32), 'Wv': jax.random.normal(ks[4], (D_MODEL, D_MODEL), jnp.float32) * s, 'bv': jax.random.normal(ks[5], (D_MODEL,), jnp.float32) * s}
    _L0_xattn_all = _L0_xattn_setup()
    _L0_xattn_in = {k: v for k, v in _L0_xattn_all.items() if k in ('Wq', 'bq', 'qk_b', 'Wv', 'bv')}
    del _L0_xattn_all

    def _L0_ffn_setup():
        import jax, jax.numpy as jnp
        import numpy as np
        DIM = 128
        DEPTH = 6
        HEADS = 16
        DIM_HEAD = 64
        WINDOW = 32
        INNER = HEADS * DIM_HEAD
        DIM_INNER = int(DIM * 4 * 2 / 3)
        QK_SCALE = 8.0

        def shift_tokens(t):
            a, s = jnp.split(t, 2, -1)
            s = jnp.pad(s, ((0, 0), (1, 0), (0, 0)))[:, :-1]
            return jnp.concatenate([a, s], -1)

        def l2norm(t):
            return t / jnp.maximum(jnp.linalg.norm(t, axis=-1, keepdims=True), 1e-12)

        def rotate_half(x):
            x1, x2 = jnp.split(x, 2, -1)
            return jnp.concatenate([-x2, x1], -1)

        def rotary_tables(n):
            half = jnp.arange(0, DIM_HEAD, 2, dtype=jnp.float32)
            inv_freq = 1.0 / 10000.0 ** (half / DIM_HEAD)
            t = jnp.arange(n, dtype=jnp.float32)
            freqs = t[:, None] * inv_freq[None, :]
            freqs = jnp.concatenate([freqs, freqs], -1)
            base_scale = (half + 0.4 * DIM_HEAD) / (1.4 * DIM_HEAD)
            power = (t - n // 2) / (WINDOW // 2)
            scale = base_scale[None, :] ** power[:, None]
            scale = jnp.concatenate([scale, scale], -1)
            return (freqs, scale)

        def local_attention(q, k, v):
            b, h, n, d = q.shape
            w = WINDOW
            nw = n // w
            bq = q.reshape(b, h, nw, w, d)
            bk = k.reshape(b, h, nw, w, d)
            bv = v.reshape(b, h, nw, w, d)

            def look(t):
                p = jnp.pad(t, ((0, 0), (0, 0), (1, 0), (0, 0), (0, 0)))
                return jnp.concatenate([p[:, :, :nw], p[:, :, 1:]], axis=3)
            bk2, bv2 = (look(bk), look(bv))
            seq = jnp.arange(n).reshape(nw, w)
            seq_p = jnp.pad(seq, ((1, 0), (0, 0)), constant_values=-1)
            jt = jnp.concatenate([seq_p[:nw], seq_p[1:]], axis=1)
            it = seq[:, :, None]
            jb = jt[:, None, :]
            mask = (it < jb) | (it > jb + w) | (jb == -1)
            sim = jnp.einsum('bhwie,bhwje->bhwij', bq, bk2) * QK_SCALE
            sim = jnp.where(mask, -jnp.finfo(sim.dtype).max, sim)
            attn = jax.nn.softmax(sim, -1)
            out = jnp.einsum('bhwij,bhwje->bhwie', attn, bv2)
            return out.reshape(b, h, n, d)

        def attn_layer(x, Wqkv, qs, ksc, Wo):
            b, n, _ = x.shape
            qkv = x @ Wqkv
            q, k, v = jnp.split(qkv, 3, -1)
            sh = lambda t: t.reshape(b, n, HEADS, DIM_HEAD).transpose(0, 2, 1, 3)
            q, k, v = (sh(q), sh(k), sh(v))
            q = l2norm(q) * qs
            k = l2norm(k) * ksc
            freqs, scale = rotary_tables(n)
            cos, sin = (jnp.cos(freqs), jnp.sin(freqs))
            q = q * cos * scale + rotate_half(q) * sin * scale
            inv = 1.0 / scale
            k = k * cos * inv + rotate_half(k) * sin * inv
            out = local_attention(q, k, v)
            out = out.transpose(0, 2, 1, 3).reshape(b, n, INNER)
            return out @ Wo

        def ffn_layer(x, g, bln, W1, b1, W2, b2):
            mu = x.mean(-1, keepdims=True)
            var = ((x - mu) ** 2).mean(-1, keepdims=True)
            xn = (x - mu) / jnp.sqrt(var + 1e-05) * g + bln
            hg = xn @ W1 + b1
            a, gate = jnp.split(hg, 2, -1)
            return a * jax.nn.gelu(gate, approximate=False) @ W2 + b2
        key = jax.random.key(seed)
        ks = jax.random.split(key, 8)
        B, N = (2, 256)
        init = lambda k, shape: jax.random.normal(k, shape, jnp.float32) * 0.02
        return {'x': jax.random.normal(ks[0], (B, N, DIM), jnp.float32), 'Wqkv': init(ks[1], (DEPTH, DIM, 3 * INNER)), 'q_scale': jnp.ones((DEPTH, DIM_HEAD), jnp.float32), 'k_scale': jnp.ones((DEPTH, DIM_HEAD), jnp.float32), 'Wo': init(ks[2], (DEPTH, INNER, DIM)), 'ln_g': jnp.ones((DEPTH, DIM), jnp.float32), 'ln_b': jnp.zeros((DEPTH, DIM), jnp.float32), 'W1': init(ks[3], (DEPTH, DIM, 2 * DIM_INNER)), 'b1': jnp.zeros((DEPTH, 2 * DIM_INNER), jnp.float32), 'W2': init(ks[4], (DEPTH, DIM_INNER, DIM)), 'b2': jnp.zeros((DEPTH, DIM), jnp.float32)}
    _L0_ffn_all = _L0_ffn_setup()
    _L0_ffn_in = {k: v for k, v in _L0_ffn_all.items() if k in ('Wqkv', 'q_scale', 'k_scale', 'Wo', 'ln_g', 'ln_b', 'W1', 'b1', 'W2', 'b2')}
    del _L0_ffn_all
    return {'x': x, 'ctx_1024': ctx_1024, 'g_xattn': g_xattn, 'g_ffn': g_ffn, 'L0_xattn_Wq': _L0_xattn_in['Wq'], 'L0_xattn_bq': _L0_xattn_in['bq'], 'L0_xattn_qk_b': _L0_xattn_in['qk_b'], 'L0_xattn_Wv': _L0_xattn_in['Wv'], 'L0_xattn_bv': _L0_xattn_in['bv'], 'L0_ffn_Wqkv': _L0_ffn_in['Wqkv'], 'L0_ffn_q_scale': _L0_ffn_in['q_scale'], 'L0_ffn_k_scale': _L0_ffn_in['k_scale'], 'L0_ffn_Wo': _L0_ffn_in['Wo'], 'L0_ffn_ln_g': _L0_ffn_in['ln_g'], 'L0_ffn_ln_b': _L0_ffn_in['ln_b'], 'L0_ffn_W1': _L0_ffn_in['W1'], 'L0_ffn_b1': _L0_ffn_in['b1'], 'L0_ffn_W2': _L0_ffn_in['W2'], 'L0_ffn_b2': _L0_ffn_in['b2']}

def reference(x, ctx_1024, g_xattn, g_ffn, L0_xattn_Wq, L0_xattn_bq, L0_xattn_qk_b, L0_xattn_Wv, L0_xattn_bv, L0_ffn_Wqkv, L0_ffn_q_scale, L0_ffn_k_scale, L0_ffn_Wo, L0_ffn_ln_g, L0_ffn_ln_b, L0_ffn_W1, L0_ffn_b1, L0_ffn_W2, L0_ffn_b2):
    import jax
    import jax.numpy as jnp

    def _L0_xattn_ref(query, value, Wq, bq, qk_b, Wv, bv):
        import jax, jax.numpy as jnp
        import numpy as np
        import math
        D_MODEL = 128
        NUM_HEADS = 16
        BATCH, SEQ = (4, 512)
        q = jnp.einsum('bsd,ed->bse', query, Wq) + bq + qk_b
        v = jnp.einsum('bsd,ed->bse', value, Wv) + bv
        inv_scale = math.sqrt(query.shape[-1] / NUM_HEADS)
        scores = jnp.einsum('bqd,bkd->bqk', q, v) / inv_scale
        attn = jax.nn.softmax(scores, axis=-1)
        return jnp.einsum('bqk,bkd->bqd', attn, v)

    def _L0_ffn_ref(x, Wqkv, q_scale, k_scale, Wo, ln_g, ln_b, W1, b1, W2, b2):
        import jax, jax.numpy as jnp
        import numpy as np
        DIM = 128
        DEPTH = 6
        HEADS = 16
        DIM_HEAD = 64
        WINDOW = 32
        INNER = HEADS * DIM_HEAD
        DIM_INNER = int(DIM * 4 * 2 / 3)
        QK_SCALE = 8.0

        def shift_tokens(t):
            a, s = jnp.split(t, 2, -1)
            s = jnp.pad(s, ((0, 0), (1, 0), (0, 0)))[:, :-1]
            return jnp.concatenate([a, s], -1)

        def l2norm(t):
            return t / jnp.maximum(jnp.linalg.norm(t, axis=-1, keepdims=True), 1e-12)

        def rotate_half(x):
            x1, x2 = jnp.split(x, 2, -1)
            return jnp.concatenate([-x2, x1], -1)

        def rotary_tables(n):
            half = jnp.arange(0, DIM_HEAD, 2, dtype=jnp.float32)
            inv_freq = 1.0 / 10000.0 ** (half / DIM_HEAD)
            t = jnp.arange(n, dtype=jnp.float32)
            freqs = t[:, None] * inv_freq[None, :]
            freqs = jnp.concatenate([freqs, freqs], -1)
            base_scale = (half + 0.4 * DIM_HEAD) / (1.4 * DIM_HEAD)
            power = (t - n // 2) / (WINDOW // 2)
            scale = base_scale[None, :] ** power[:, None]
            scale = jnp.concatenate([scale, scale], -1)
            return (freqs, scale)

        def local_attention(q, k, v):
            b, h, n, d = q.shape
            w = WINDOW
            nw = n // w
            bq = q.reshape(b, h, nw, w, d)
            bk = k.reshape(b, h, nw, w, d)
            bv = v.reshape(b, h, nw, w, d)

            def look(t):
                p = jnp.pad(t, ((0, 0), (0, 0), (1, 0), (0, 0), (0, 0)))
                return jnp.concatenate([p[:, :, :nw], p[:, :, 1:]], axis=3)
            bk2, bv2 = (look(bk), look(bv))
            seq = jnp.arange(n).reshape(nw, w)
            seq_p = jnp.pad(seq, ((1, 0), (0, 0)), constant_values=-1)
            jt = jnp.concatenate([seq_p[:nw], seq_p[1:]], axis=1)
            it = seq[:, :, None]
            jb = jt[:, None, :]
            mask = (it < jb) | (it > jb + w) | (jb == -1)
            sim = jnp.einsum('bhwie,bhwje->bhwij', bq, bk2) * QK_SCALE
            sim = jnp.where(mask, -jnp.finfo(sim.dtype).max, sim)
            attn = jax.nn.softmax(sim, -1)
            out = jnp.einsum('bhwij,bhwje->bhwie', attn, bv2)
            return out.reshape(b, h, n, d)

        def attn_layer(x, Wqkv, qs, ksc, Wo):
            b, n, _ = x.shape
            qkv = x @ Wqkv
            q, k, v = jnp.split(qkv, 3, -1)
            sh = lambda t: t.reshape(b, n, HEADS, DIM_HEAD).transpose(0, 2, 1, 3)
            q, k, v = (sh(q), sh(k), sh(v))
            q = l2norm(q) * qs
            k = l2norm(k) * ksc
            freqs, scale = rotary_tables(n)
            cos, sin = (jnp.cos(freqs), jnp.sin(freqs))
            q = q * cos * scale + rotate_half(q) * sin * scale
            inv = 1.0 / scale
            k = k * cos * inv + rotate_half(k) * sin * inv
            out = local_attention(q, k, v)
            out = out.transpose(0, 2, 1, 3).reshape(b, n, INNER)
            return out @ Wo

        def ffn_layer(x, g, bln, W1, b1, W2, b2):
            mu = x.mean(-1, keepdims=True)
            var = ((x - mu) ** 2).mean(-1, keepdims=True)
            xn = (x - mu) / jnp.sqrt(var + 1e-05) * g + bln
            hg = xn @ W1 + b1
            a, gate = jnp.split(hg, 2, -1)
            return a * jax.nn.gelu(gate, approximate=False) @ W2 + b2
        for i in range(DEPTH):
            x = attn_layer(shift_tokens(x), Wqkv[i], q_scale[i], k_scale[i], Wo[i]) + x
            x = ffn_layer(shift_tokens(x), ln_g[i], ln_b[i], W1[i], b1[i], W2[i], b2[i]) + x
        return x
    x = x + jnp.tanh(g_xattn[0]) * _L0_xattn_ref(_layernorm(x, axis=-1), ctx_1024, L0_xattn_Wq, L0_xattn_bq, L0_xattn_qk_b, L0_xattn_Wv, L0_xattn_bv)
    x = x + jnp.tanh(g_ffn[0]) * _L0_ffn_ref(_layernorm(x, axis=-1), L0_ffn_Wqkv, L0_ffn_q_scale, L0_ffn_k_scale, L0_ffn_Wo, L0_ffn_ln_g, L0_ffn_ln_b, L0_ffn_W1, L0_ffn_b1, L0_ffn_W2, L0_ffn_b2)
    return x

_drawn_inputs = setup_inputs


def setup_inputs(seed=0):
    import zlib

    import numpy as np

    out = dict(_drawn_inputs(seed))
    spreads = {'L0_xattn_qk_b': (0.0, 0.1),
     'L0_ffn_q_scale': (1.0, 0.2),
     'L0_ffn_k_scale': (1.0, 0.599),
     'L0_ffn_ln_g': (1.0, 0.6),
     'L0_ffn_ln_b': (0.0, 0.8),
     'L0_ffn_b1': (0.0, 0.1),
     'L0_ffn_b2': (0.0, 0.1)}
    factors = {}
    for name, (base, spread) in spreads.items():
        noise = np.random.default_rng([zlib.crc32(name.encode()), seed]).standard_normal(out[name].shape)
        drawn = base * np.exp(spread * noise) if base else spread * noise
        out[name] = jnp.asarray(drawn.astype(out[name].dtype))
    for name, factor in factors.items():
        out[name] = (out[name] * factor).astype(out[name].dtype)
    return out
```

```python
import numpy as np
import concourse.bass as bass
from concourse import mybir
from contextlib import ExitStack

L, NB, S, D = 6, 16, 128, 128
HEADS, DH, WINDOW = 16, 64, 32
INNER = HEADS * DH
DI = int(D * 4 * 2 / 3)
HC = 512 // DH
NCH = 2 * INNER // 512
CHUNK_AT = [0, INNER, 512, INNER + 512, 2 * INNER, 2 * INNER + 512]
WO_AT = 3 * INNER
W1_AT = WO_AT + (INNER // 128) * D
W2_AT = W1_AT + 2 * DI
KT2 = -(-DI // 128)
W_SIZE = W2_AT + KT2 * D
START = 16
GB = 4
CROSS_HEADS = 16
NEG = -1e30
SS_SCALE_LOG2 = 20


def program(nc, x, ctxT, g_xattn, g_ffn, Wq, bq, qk_b, Wv, bv, Wqkv, q_scale, k_scale, Wo, ln_g, ln_b, W1, b1, W2,
            b2, rot_cos, rot_sin, band, eye, shift, out):
    F32, BF16 = mybir.dt.float32, mybir.dt.bfloat16
    ALU, ACT, AX = mybir.AluOpType, mybir.ActivationFunctionType, mybir.AxisListType.X
    ds = bass.ds
    es = ExitStack()

    def sb(name, shape, dt=F32):
        return es.enter_context(nc.sbuf_tensor(name, shape, dt))

    def sem(name):
        return es.enter_context(nc.semaphore(name))

    with es:
        H = sb("H", [128, NB, D])
        X1 = sb("X1", [128, NB, D])
        XhT = sb("XhT", [128, NB, S])
        WB = sb("WB", [128, 2 * W_SIZE])
        B1 = sb("B1", [128, L, 2 * DI])
        B2 = sb("B2", [128, L, D])
        TC = sb("TC", [128, L, 2, DH])
        TS = sb("TS", [128, L, 2, DH])
        rc = sb("rc", [128, 2, DH])
        rsn = sb("rsn", [128, 2, DH])
        qs = sb("qs", [128, 2, L, DH])
        ident = sb("ident", [128, 128])
        shf = sb("shf", [128, 128])
        identb = sb("identb", [128, 128], BF16)
        maskf = sb("maskf", [128, 128])
        maskb = sb("maskb", [128, 128], BF16)
        gate2 = sb("gate2", [128, 2])
        tg = sb("tg", [128, 2])
        lng = sb("lng", [128, L])
        lnb = sb("lnb", [128, L])
        wqT = sb("wqT", [128, 128])
        wvT = sb("wvT", [128, 128])
        bqc = sb("bqc", [128, 3])
        bqs = sb("bqs", [128, 1])
        bvb = sb("bvb", [128, 128])
        xw = sb("xw", [128, 2, D])
        xsT = sb("xsT", [128, 2, S])
        sq = sb("sq", [128, 2, 512])
        ss = sb("ss", [128, 2, 4 * HC])
        ssc = sb("ssc", [128, 2, 4 * HC])
        lnv = sb("lnv", [128, 2, 4 * HC])
        rn = sb("rn", [128, 2, 4 * HC])
        u = sb("u", [128, 2, NCH, 512])
        t2 = sb("t2", [128, 2, 512])
        qkT = sb("qkT", [128, NCH, 4, 128])
        nm = sb("nm", [128, 16])
        sm = sb("sm", [128, 16])
        rs = sb("rs", [128, 16])
        P = sb("P", [128, 4, 4, 128])
        PT = sb("PT", [128, 2, 4, 128])
        v = sb("v", [128, 2, INNER])
        OT = sb("OT", [128, 2, 2, 4, 128])
        bst = sb("bst", [128, 2, 6])
        mv = sb("mv", [128, 2, 2])
        lv = sb("lv", [128, 2])
        rstd = sb("rstd", [128, 2])
        xh = sb("xh", [128, 2, D])
        xf = sb("xf", [128, 2, S])
        gt = sb("gt", [128, 2, DI])
        at_ = sb("at", [128, 2, DI])
        hh = sb("hh", [128, 2, DI])
        hT = sb("hT", [128, 2, KT2, 128])
        yb = sb("yb", [128, 2, D])
        cT = t2[:, 0, :]
        xh4, xhT4, qT4, vT4 = (u[:, 0, j, :] for j in range(4))
        p4, pT4, v4, out4 = (u[:, 1, j, :] for j in range(4))
        st4 = sb("st4", [128, GB, 6])
        mv4 = sb("mv4", [128, GB, 2])
        lv4 = sb("lv4", [128, GB])
        rstd4 = sb("rstd4", [128, GB])
        mx4 = sb("mx4", [128, GB])
        nm4 = sb("nm4", [128, GB])
        sum4 = sb("sum4", [128, GB])
        rc4 = sb("rc4", [128, GB])
        rg4 = sb("rg4", [128, GB])
        cols = sb("cols", [128, 2])
        eps_col, exp_col = cols[:, 0:1], cols[:, 1:2]

        def bank(name):
            return es.enter_context(nc.psum_tensor("bank_" + name, [128, 512], F32))

        A = [bank("A0"), bank("A1")]
        B = [bank("B0"), bank("B1")]
        C = [bank("C0"), bank("C1")]
        Dk = bank("D")
        E = bank("E")

        in_ready, w_ready, out_done = sem("in_ready"), sem("w_ready"), sem("out_done")
        PE_SEMS = A_full, B_full, C_full, pv_done, Wo_done, xT_done, xs_done, xhT_done, y_done = [
            sem(s) for s in ("A_full", "B_full", "C_full", "pv_done", "Wo_done", "xT_done", "xs_done", "xhT_done",
                             "y_done")]
        DVE_SEMS = A_out, C_out, ss_done, ss_ready, mx_done, sum_done, rs_ready, res_done, bst_done, mv_ready, \
            xh_ready, hh_ready, y2_done = [
                sem(s) for s in ("A_out", "C_out", "ss_done", "ss_ready", "mx_done", "sum_done", "rs_ready",
                                 "res_done", "bst_done", "mv_ready", "xh_ready", "hh_ready",
                                 "y2_done")]
        ACT_SEMS = B_out, D_out, sq_done, exp_done, xsT_ready, ln_done, rn_ready, lv_done, rstd_ready, xhT_ready, \
            gelu_done = [
                sem(s) for s in ("B_out", "D_out", "sq_done", "exp_done", "xsT_ready", "ln_done", "rn_ready",
                                 "lv_done", "rstd_ready", "xhT_ready", "gelu_done")]
        POOL_SEMS = xw_ready, add_done, qk_ready, P_ready, xf_ready = [
            sem(s) for s in ("xw_ready", "add_done", "qk_ready", "P_ready", "xf_ready")]
        h_ready = sem("h_ready")
        tables_ready, tanh_done, consts_done = sem("tables_ready"), sem("tanh_done"), sem("consts_done")
        bqs_ready, consts_act = sem("bqs_ready"), sem("consts_act")
        c_st, c_mv, c_lv, c_rstd, c_xh, c_ctx = (sem(s) for s in ("c_st", "c_mv", "c_lv", "c_rstd", "c_xh", "c_ctx"))
        c_xT, c_xTs, c_qv, c_v, c_qvs, c_vs = (sem(s) for s in ("c_xT", "c_xTs", "c_qv", "c_v", "c_qvs", "c_vs"))
        c_sc, c_mx, c_nm, c_exp, c_rc, c_rg, c_pT, c_pTs, c_o, c_x1 = (
            sem(s) for s in ("c_sc", "c_mx", "c_nm", "c_exp", "c_rc", "c_rg", "c_pT", "c_pTs", "c_o", "c_x1"))
        fin_ready = sem("fin_ready")
        wait_met = sem("wait_met")

        def n_(l, b):
            return l * NB + b + START

        def nk(l, b, per, k):
            return l * (NB * per) + b * per + k + START

        A_PER, B_PER, C_PER = NB * 6 + NB, NB * 8 + NB, NB * 4 + NB

        def a_at(l, b, c):
            return l * A_PER + b * 6 + c + START

        def b_at(l, b, j):
            return l * B_PER + b * 8 + j + START

        def c_at(l, b, g):
            return l * C_PER + b * 4 + g + START

        def b_before(l, b, back, k):
            if isinstance(b, int) and b < back:
                return l * B_PER - NB + START
            return b_at(l, b - back, k)

        def ffn_at(l, b, par, j):
            return l * A_PER + NB * 6 + b + j + START if par == 0 else l * C_PER + NB * 4 + b - 1 + j + START

        def attention_pipeline(eng, l, step):
            step(l, 0, 0, True, False, False)
            step(l, 1, 1, True, True, False)
            with eng.Fori(1, NB // 2) as pair:
                step(l, pair * 2, 0, True, True, True)
                step(l, pair * 2 + 1, 1, True, True, True)
            step(l, NB, 0, False, True, True)
            step(l, NB + 1, 1, False, False, True)

        def ffn_pipeline(eng, l, step):
            step(l, 0, 0, True, False)
            with eng.Fori(0, NB // 2 - 1) as pair:
                step(l, pair * 2 + 1, 1, True, True)
                step(l, pair * 2 + 2, 0, True, True)
            step(l, NB - 1, 1, True, True)
            step(l, NB, 0, False, True)

        def heads(ap, n=HC):
            return ap.rearrange("p (h a d) -> p h a d", h=n, a=2)

        N_SMALL = 19
        N_INPUTS = N_SMALL + 2
        block = es.enter_context(nc.Block())

        @block.sync
        def _(sp):
            sp.dma_start(H[:], x.rearrange("b s d -> s b d")).then_inc(in_ready, 16)
            sp.dma_start(XhT[:], ctxT.rearrange("b d s -> d b s")).then_inc(in_ready, 16)
            small = [
                (ident[:], eye), (shf[:], shift), (maskf[:], band), (rc[:], rot_cos), (rsn[:], rot_sin),
                (wqT[:], Wq), (wvT[:], Wv),
                (bqc[:, 0:1], bq.rearrange("(p o) -> p o", o=1)), (bqc[:, 1:2], qk_b.rearrange("(p o) -> p o", o=1)),
                (bqc[:, 2:3], bv.rearrange("(p o) -> p o", o=1)),
                (bvb[:], bv.partition_broadcast(128)),
                (gate2[:, 0:1], g_xattn.partition_broadcast(128)), (gate2[:, 1:2], g_ffn.partition_broadcast(128)),
                (qs[:, 0], q_scale.partition_broadcast(128)), (qs[:, 1], k_scale.partition_broadcast(128)),
                (lng[:], ln_g), (lnb[:], ln_b),
                (B2[:], b2.partition_broadcast(128)), (B1[:], b1.partition_broadcast(128)),
            ]
            assert len(small) == N_SMALL
            for dst, src in small:
                sp.dma_start(dst, src).then_inc(in_ready, 16)
            for l in range(L):
                if l >= 1:
                    sp.wait_ge(w_ready, 80 * l)
                if l >= 2:
                    sp.wait_ge(h_ready, NB * l + START)
                o = (l % 2) * W_SIZE
                sp.dma_start(WB[:, o:o + WO_AT], Wqkv[l]).then_inc(w_ready, 16)
                sp.dma_start(WB[:, o + WO_AT:o + W1_AT].rearrange("p (k n) -> p k n", n=D),
                             Wo[l].rearrange("(k p) n -> p k n", p=128)).then_inc(w_ready, 16)
                sp.dma_start(WB[:, o + W1_AT:o + W2_AT], W1[l]).then_inc(w_ready, 16)
                sp.dma_start(WB[:, o + W2_AT:o + W2_AT + (KT2 - 1) * D].rearrange("p (k n) -> p k n", n=D),
                             W2[l, 0:(KT2 - 1) * 128].rearrange("(k p) n -> p k n", p=128)).then_inc(w_ready, 16)
                sp.dma_start(WB[0:DI - (KT2 - 1) * 128, o + W2_AT + (KT2 - 1) * D:o + W_SIZE],
                             W2[l, (KT2 - 1) * 128:DI]).then_inc(w_ready, 16)
            for q in range(4):
                sp.wait_ge(fin_ready, q + 1)
                sp.dma_start(out[4 * q:4 * q + 4].rearrange("b s d -> s b d"),
                             X1[:, 4 * q:4 * q + 4]).then_inc(out_done, 16)
            sp.wait_ge(out_done, 64)

        @block.gpsimd
        def _(pool):
            for s in POOL_SEMS:
                pool.sem_inc(s, START)

            def attention_step(l, it, par, project, attend, finish):
                n, a = it, it - 1
                if project:
                    pool.wait_ge(h_ready, n_(l, n) + 1)
                    pool.wait_ge(xT_done, n_(l, n) - 1)
                    pool.sem_inc(wait_met, 1)
                    nc.gpsimd.tensor_copy(xw[:, par], H[:, ds(n, 1)].rearrange("p o d -> p (o d)")).then_inc(xw_ready, 1)

                def add(c):
                    pool.wait_ge(A_out, a_at(l, n, c) + 1)
                    nc.gpsimd.tensor_tensor(u[:, par, c], u[:, par, c], t2[:, c % 2], ALU.add).then_inc(add_done, 1)

                def normalise(g):
                    pool.wait_ge(rs_ready, nk(l, a, 4, g) + 1)
                    nc.gpsimd.tensor_tensor(P[:, g], P[:, g], rs[:, 4 * g:4 * g + 4].unsqueeze(2).broadcast_to([128, 4, 128]),
                                            ALU.mult).then_inc(P_ready, 1)
                if project:
                    add(0)
                    add(1)
                if attend:
                    normalise(0)
                    normalise(1)
                if project:
                    add(2)
                if attend:
                    normalise(2)
                    normalise(3)
                if project:
                    add(3)
                    pool.wait_ge(rn_ready, n_(l, n) + 1)
                    for c in range(NCH):
                        pool.wait_ge(add_done, nk(l, n, 4, c) + 1)
                        uc = u[:, par, c].rearrange("p (h d) -> p h d", h=HC)
                        nc.gpsimd.tensor_tensor(uc, uc, rn[:, par, HC * c:HC * c + HC].unsqueeze(2).broadcast_to([128, HC, DH]),
                                                ALU.mult).then_inc(qk_ready, 1)

            def ffn_step(l, it, par, up, down):
                if up:
                    pool.wait_ge(xhT_ready, n_(l, it) + 1)
                    pool.wait_ge(A_full if par == 0 else C_full, ffn_at(l, it, par, 0))
                    pool.sem_inc(wait_met, 1)
                    nc.gpsimd.tensor_copy(xf[:, par], XhT[:, ds(it, 1)].rearrange("p o d -> p (o d)")).then_inc(xf_ready, 1)

            pool.wait_ge(in_ready, 16 * N_INPUTS)
            pool.sem_inc(c_ctx, START)
            with pool.Fori(0, NB // GB) as g:
                pool.wait_ge(c_v, g + START)
                pool.sem_inc(wait_met, 1)
                nc.gpsimd.tensor_copy(cT, XhT[:, ds(g * GB, GB)].rearrange("p b d -> p (b d)")).then_inc(c_ctx, 1)
            with pool.Fori(0, L) as l:
                attention_pipeline(pool, l, attention_step)
                ffn_pipeline(pool, l, ffn_step)

        @block.scalar
        def _(act):
            for s in ACT_SEMS + [c_lv, c_rstd, c_xTs, c_qvs, c_exp, c_pTs]:
                act.sem_inc(s, START)
            act.wait_ge(in_ready, 16 * N_INPUTS)
            nc.scalar.activation(tg[:], gate2[:], ACT.Tanh).then_inc(tanh_done, 1)
            nc.scalar.copy(identb[:], ident[:]).then_inc(consts_act, 1)
            nc.scalar.copy(maskb[:], maskf[:]).then_inc(consts_act, 1)
            nc.scalar.preload_act_table_set("natural_log_exp_and_others")

            def cross_rstd(k):
                act.wait_ge(c_mv, k + 1)
                nc.scalar.activation(lv4[:], mv4[:, :, 1], ACT.Ln, bias=eps_col).then_inc(c_lv, 1)
                act.wait_ge(c_lv, k + 1)
                nc.scalar.activation(rstd4[:], lv4[:], ACT.Exp, scale=-0.5).then_inc(c_rstd, 1)

            act.wait_ge(consts_done, 1)
            act.wait_ge(bqs_ready, 1)
            with act.Fori(0, NB // GB) as g:
                cross_rstd(g * 2 + START)
                act.wait_ge(c_xT, g + 1 + START)
                nc.scalar.copy(xhT4, A[0][:]).then_inc(c_xTs, 1)
                act.wait_ge(c_qv, g + 1 + START)
                nc.scalar.activation(qT4, C[0][:], ACT.Identity, bias=bqs[:])
                nc.scalar.activation(vT4, C[1][:], ACT.Identity, bias=bqc[:, 2:3]).then_inc(c_qvs, 1)
                act.wait_ge(c_nm, g + 1 + START)
                for j in range(GB):
                    i = nc.scalar.activation(p4[:, 128 * j:128 * j + 128], B[1][:, 128 * j:128 * j + 128], ACT.Exp,
                                             bias=nm4[:, j:j + 1], scale=(D / CROSS_HEADS) ** -0.5,
                                             accum_out=sum4[:, j:j + 1])
                i.then_inc(c_exp, 1)
                act.wait_ge(c_pT, g + 1 + START)
                nc.scalar.copy(pT4, A[0][:]).then_inc(c_pTs, 1)
                cross_rstd(g * 2 + 1 + START)

            def attention_step(l, it, par, project, attend, finish):
                n, a, m = it, it - 1, it - 2

                def qk_out(g):
                    act.wait_ge(B_full, b_at(l, a, g) + 1)
                    act.wait_ge(C_full, c_at(l, a, 0) - (2 if g < 2 else 0) if not (isinstance(a, int) and a < 1)
                                else c_at(l, 0, 0) - NB)
                    nc.scalar.copy(qkT[:, g].rearrange("p t n -> p (t n)"), B[g % 2][:]).then_inc(B_out, 1)

                def square(c):
                    act.wait_ge(A_full, a_at(l, n, c) + 1)
                    act.wait_ge(ss_done, nk(l, n, 4, c) - 1)
                    nc.scalar.activation(sq[:, c % 2], A[c % 2][:], ACT.Square).then_inc(sq_done, 1)

                def exp(g):
                    act.wait_ge(C_out, c_at(l, a, g) + 1)
                    pg = P[:, g].rearrange("p h k -> p (h k)")
                    nc.scalar.activation(pg, pg, ACT.Exp).then_inc(exp_done, 1)

                def p_out(g):
                    act.wait_ge(B_full, b_at(l, a, 4 + g) + 1)
                    act.wait_ge(pv_done, nk(l, a, 4, g) - 1)
                    nc.scalar.copy(PT[:, g % 2].rearrange("p h k -> p (h k)"), B[g % 2][:]).then_inc(B_out, 1)

                def o_out(s):
                    act.wait_ge(pv_done, nk(l, a, 4, 2 * s + 2))
                    act.wait_ge(Wo_done, n_(l, a) - 1)
                    nc.scalar.copy(OT[:, 1 - par, s].rearrange("p t n -> p (t n)"), Dk[:]).then_inc(D_out, 1)

                if project:
                    act.wait_ge(xT_done, n_(l, n) + 1)
                    act.wait_ge(A_full, a_at(l, n - 2, 6) if not isinstance(n, int) else l * A_PER - NB + START)
                    nc.scalar.copy(xsT[0:64, par], E[0:64, 0:S])
                    nc.scalar.copy(xsT[64:128, par, 1:S], E[64:128, 0:S - 1]).then_inc(xsT_ready, 1)
                if attend:
                    qk_out(0)
                    qk_out(1)
                if project:
                    square(0)
                if attend:
                    qk_out(2)
                    qk_out(3)
                    exp(0)
                    exp(1)
                if project:
                    square(1)
                if finish:
                    act.wait_ge(mv_ready, n_(l, m) + 1)
                    nc.scalar.activation(lv[:, par:par + 1], mv[:, par, 1:2], ACT.Ln, bias=eps_col).then_inc(lv_done, 1)
                    act.wait_ge(lv_done, n_(l, m) + 1)
                    act.wait_ge(xh_ready, n_(l, m) - 1)
                    nc.scalar.activation(rstd[:, par:par + 1], lv[:, par:par + 1], ACT.Exp, scale=-0.5).then_inc(rstd_ready, 1)
                if attend:
                    exp(2)
                    exp(3)
                if project:
                    square(2)
                if attend:
                    p_out(0)
                    p_out(1)
                if project:
                    square(3)
                if finish:
                    act.wait_ge(xhT_done, n_(l, m) + 1)
                    act.sem_inc(wait_met, 1)
                    nc.scalar.activation(XhT[:, ds(m, 1)].rearrange("p o d -> p (o d)"), E[:, 0:S], ACT.Identity,
                                         scale=lng[:, ds(l, 1)], bias=lnb[:, ds(l, 1)]).then_inc(xhT_ready, 1)
                if attend:
                    o_out(0)
                    p_out(2)
                    p_out(3)
                if project:
                    act.wait_ge(ss_ready, n_(l, n) + 1)
                    nc.scalar.activation(lnv[:, par], ssc[:, par], ACT.Ln, scale=float(2 ** SS_SCALE_LOG2)).then_inc(ln_done, 1)
                    act.wait_ge(ln_done, n_(l, n) + 1)
                    act.wait_ge(qk_ready, nk(l, n, 4, -4))
                    nc.scalar.activation(rn[:, par], lnv[:, par], ACT.Exp, scale=-0.5, bias=exp_col).then_inc(rn_ready, 1)
                if attend:
                    o_out(1)

            def ffn_step(l, it, par, up, down):
                if up:
                    act.wait_ge(A_out if par == 0 else C_out, ffn_at(l, it, par, 0) + 1)
                    nc.scalar.activation(gt[:, par], gt[:, par], ACT.Gelu).then_inc(gelu_done, 1)
                if down:
                    m, mp = it - 1, 1 - par
                    act.wait_ge(B_full, l * B_PER + NB * 8 + m + 1 + START)
                    act.wait_ge(y_done, n_(l, m) - 1)
                    nc.scalar.copy(hT[:, mp, 0:KT2 - 1].rearrange("p t n -> p (t n)"), B[mp][:, 0:(KT2 - 1) * 128])
                    nc.scalar.copy(hT[0:DI - (KT2 - 1) * 128, mp, KT2 - 1],
                                   B[mp][0:DI - (KT2 - 1) * 128, (KT2 - 1) * 128:KT2 * 128]).then_inc(B_out, 1)

            with act.Fori(0, L) as l:
                nc.scalar.preload_act_table_set("natural_log_exp_and_others")
                attention_pipeline(act, l, attention_step)
                nc.scalar.preload_act_table(ACT.Gelu)
                ffn_pipeline(act, l, ffn_step)

        @block.vector
        def _(dve):
            for s in DVE_SEMS + [c_st, c_mv, c_xh, c_vs, c_mx, c_nm, c_rc, c_rg, c_x1, h_ready]:
                dve.sem_inc(s, START)
            nc.vector.memset(eps_col, 1e-5)
            nc.vector.memset(exp_col, 0.5 * SS_SCALE_LOG2 * float(np.log(2.0)))
            nc.vector.memset(xsT[64:128, :, 0:1], 0.0).then_inc(consts_done, 1)
            dve.wait_ge(in_ready, 16 * N_INPUTS)
            nc.vector.tensor_tensor(bqs[:], bqc[:, 0:1], bqc[:, 1:2], ALU.add).then_inc(bqs_ready, 1)
            for w in range(2):
                nc.vector.tensor_tensor(TC[:, :, w], qs[:, w], rc[:, w].unsqueeze(1).broadcast_to([128, L, DH]), ALU.mult)
                for a in range(2):
                    o, i = 32 * a, 32 * (1 - a)
                    nc.vector.tensor_tensor(TS[:, :, w, o:o + 32], qs[:, w, :, i:i + 32],
                                            rsn[:, w, o:o + 32].unsqueeze(1).broadcast_to([128, L, 32]),
                                            ALU.mult).then_inc(tables_ready, 1)

            def group_norm(k, src, dst, done):
                for j in range(GB):
                    i = nc.vector.bn_stats(st4[:, j], src(j))
                i.then_inc(c_st, 1)
                dve.wait_ge(c_st, k + 1)
                dve.sem_inc(wait_met, 1)
                for j in range(GB):
                    i = nc.vector.bn_aggr(mv4[:, j], st4[:, j])
                i.then_inc(c_mv, 1)
                dve.wait_ge(c_rstd, k + 1)
                for j in range(GB):
                    dve.wait_ge(c_mv, k + 1)
                    i = nc.vector.tensor_scalar(dst(j), src(j), mv4[:, j, 0:1], rstd4[:, j:j + 1], ALU.subtract, ALU.mult)
                i.then_inc(done[0], done[1])

            with dve.Fori(0, NB // GB) as g:
                def row(t, j):
                    return t[:, ds(g * GB + j, 1)].rearrange("p o d -> p (o d)")
                dve.wait_ge(c_xT, g + START)
                dve.sem_inc(wait_met, 1)
                group_norm(g * 2 + START, lambda j: row(H, j), lambda j: xh4[:, 128 * j:128 * j + 128], (c_xh, 1))
                dve.wait_ge(c_v, g + 1 + START)
                nc.vector.tensor_tensor(v4.rearrange("p (b d) -> p b d", b=GB), B[0][:].rearrange("p (b d) -> p b d", b=GB),
                                        bvb[:].unsqueeze(1).broadcast_to([128, GB, D]), ALU.add).then_inc(c_vs, 1)
                dve.wait_ge(c_sc, g + 1 + START)
                nc.vector.tensor_reduce(mx4[:], B[1][:].rearrange("p (b d) -> p b d", b=GB), AX, ALU.max).then_inc(c_mx, 1)
                dve.wait_ge(c_mx, g + 1 + START)
                nc.vector.tensor_scalar_mul(nm4[:], mx4[:], -(D / CROSS_HEADS) ** -0.5).then_inc(c_nm, 1)
                dve.wait_ge(c_exp, g + 1 + START)
                nc.vector.reciprocal(rc4[:], sum4[:]).then_inc(c_rc, 1)
                dve.wait_ge(c_rc, g + 1 + START)
                dve.wait_ge(tanh_done, 1)
                nc.vector.tensor_scalar_mul(rg4[:], rc4[:], tg[:, 0:1]).then_inc(c_rg, 1)
                dve.wait_ge(c_rg, g + 1 + START)
                dve.wait_ge(c_o, g + 1 + START)
                for j in range(GB):
                    i = nc.vector.scalar_tensor_tensor(out=row(X1, j), in0=A[1][:, 128 * j:128 * j + 128],
                                                       scalar=rg4[:, j:j + 1], in1=row(H, j), op0=ALU.mult, op1=ALU.add)
                i.then_inc(c_x1, 1)
                dve.wait_ge(c_x1, g + 1 + START)
                dve.sem_inc(wait_met, 1)
                group_norm(g * 2 + 1 + START, lambda j: row(X1, j), lambda j: row(H, j), (h_ready, GB))
            dve.wait_ge(tables_ready, 4)

            def attention_step(l, it, par, project, attend, finish):
                n, a, m = it, it - 1, it - 2

                def rotate(c):
                    w = c % 2
                    dve.wait_ge(sq_done, nk(l, n, 4, c) + 1)
                    nc.vector.tensor_reduce(ss[:, par, HC * c:HC * c + HC], sq[:, c % 2].rearrange("p (h d) -> p h d", h=HC),
                                            AX, ALU.add).then_inc(ss_done, 1)
                    dve.wait_ge(B_full, b_before(l, n, 2, c + 1))
                    dve.wait_ge(qk_ready, nk(l, n, 4, c - 7))
                    nc.vector.tensor_tensor(u[:, par, c].rearrange("p (h d) -> p h d", h=HC),
                                            A[c % 2][:].rearrange("p (h d) -> p h d", h=HC),
                                            TC[:, ds(l, 1), w].broadcast_to([128, HC, DH]), ALU.mult)
                    dve.wait_ge(add_done, nk(l, n, 4, c) - 1)
                    nc.vector.tensor_tensor(heads(t2[:, c % 2]), heads(A[c % 2][:])[:, :, ::-1, :],
                                            TS[:, ds(l, 1), w].broadcast_to([128, HC, DH]).rearrange("p h (a d) -> p h a d", a=2),
                                            ALU.mult).then_inc(A_out, 1)

                def v_out(c):
                    dve.wait_ge(A_full, a_at(l, n, c) + 1)
                    dve.wait_ge(pv_done, nk(l, n, 4, -4))
                    nc.vector.tensor_copy(v[:, par, 512 * (c - 4):512 * (c - 3)], A[c % 2][:]).then_inc(A_out, 1)

                def softmax_max(s):
                    for g in (2 * s, 2 * s + 1):
                        dve.wait_ge(C_full, c_at(l, a, g) + 1)
                        nc.vector.tensor_reduce(nm[:, 4 * g:4 * g + 4], C[g % 2][:].rearrange("p (h k) -> p h k", h=4),
                                                AX, ALU.max).then_inc(mx_done, 1)
                    for g in (2 * s, 2 * s + 1):
                        dve.wait_ge(mx_done, nk(l, a, 4, g) + 1)
                        dve.wait_ge(B_full, b_before(l, a, 1, 4 + g + 1))
                        nc.vector.tensor_tensor(P[:, g], C[g % 2][:].rearrange("p (h k) -> p h k", h=4),
                                                nm[:, 4 * g:4 * g + 4].unsqueeze(2).broadcast_to([128, 4, 128]),
                                                ALU.subtract).then_inc(C_out, 1)

                def softmax_sum(s):
                    for g in (2 * s, 2 * s + 1):
                        dve.wait_ge(exp_done, nk(l, a, 4, g) + 1)
                        nc.vector.tensor_reduce(sm[:, 4 * g:4 * g + 4], P[:, g], AX, ALU.add).then_inc(sum_done, 1)
                    for g in (2 * s, 2 * s + 1):
                        dve.wait_ge(sum_done, nk(l, a, 4, g) + 1)
                        dve.wait_ge(P_ready, nk(l, a, 4, g) - 3)
                        nc.vector.reciprocal(rs[:, 4 * g:4 * g + 4], sm[:, 4 * g:4 * g + 4]).then_inc(rs_ready, 1)

                if finish:
                    dve.wait_ge(Wo_done, n_(l, m) + 1)
                    hm = H[:, ds(m, 1)].rearrange("p o d -> p (o d)")
                    nc.vector.tensor_tensor(hm, E[:, 0:D], hm, ALU.add).then_inc(res_done, 1)
                if project:
                    rotate(0)
                if attend:
                    softmax_max(0)
                if project:
                    rotate(1)
                if attend:
                    softmax_sum(0)
                if finish:
                    dve.wait_ge(xs_done, n_(l, m) + 1)
                    nc.vector.bn_stats(bst[:, par], E[:, 0:D]).then_inc(bst_done, 1)
                    dve.wait_ge(bst_done, n_(l, m) + 1)
                    dve.wait_ge(lv_done, n_(l, m) - 1)
                    dve.sem_inc(wait_met, 1)
                    nc.vector.bn_aggr(mv[:, par], bst[:, par]).then_inc(mv_ready, 1)
                if attend:
                    softmax_max(1)
                if project:
                    rotate(2)
                if attend:
                    softmax_sum(1)
                if finish:
                    dve.wait_ge(rstd_ready, n_(l, m) + 1)
                    dve.wait_ge(mv_ready, n_(l, m) + 1)
                    dve.wait_ge(xhT_done, n_(l, m) - 1)
                    nc.vector.tensor_scalar(xh[:, par], E[:, 0:D], mv[:, par, 0:1], rstd[:, par:par + 1], ALU.subtract,
                                            ALU.mult).then_inc(xh_ready, 1)
                if project:
                    rotate(3)
                    dve.wait_ge(ss_done, nk(l, n, 4, 4))
                    dve.wait_ge(ln_done, n_(l, n) - 1)
                    nc.vector.tensor_scalar_max(ssc[:, par], ss[:, par], 1e-24).then_inc(ss_ready, 1)
                    v_out(4)
                    v_out(5)

            def ffn_step(l, it, par, up, down):
                if up:
                    n = it
                    X, full, done = (A, A_full, A_out) if par == 0 else (C, C_full, C_out)
                    dve.wait_ge(full, ffn_at(l, n, par, 0) + 1)
                    dve.wait_ge(hh_ready, n_(l, n) - 1)
                    nc.vector.tensor_tensor(gt[:, par], X[0][:, 0:DI], B1[:, ds(l, 1), DI:2 * DI].rearrange("p o d -> p (o d)"),
                                            ALU.add).then_inc(done, 1)
                    dve.wait_ge(full, ffn_at(l, n, par, 1) + 1)
                    nc.vector.tensor_tensor(at_[:, par], X[1][:, 0:DI], B1[:, ds(l, 1), 0:DI].rearrange("p o d -> p (o d)"),
                                            ALU.add).then_inc(done, 1)
                    dve.wait_ge(done, ffn_at(l, n, par, 1) + 1)
                    dve.wait_ge(gelu_done, n_(l, n) + 1)
                    dve.wait_ge(B_full, l * B_PER + NB * 8 + n - 1 + START)
                    nc.vector.tensor_tensor(hh[:, par], at_[:, par], gt[:, par], ALU.mult).then_inc(hh_ready, 1)
                if down:
                    m, mp = it - 1, 1 - par
                    dve.wait_ge(y_done, n_(l, m) + 1)
                    hm = H[:, ds(m, 1)].rearrange("p o d -> p (o d)")
                    nc.vector.tensor_tensor(yb[:, mp], Dk[:, 0:D], B2[:, ds(l, 1)].rearrange("p o d -> p (o d)"),
                                            ALU.add).then_inc(y2_done, 1)
                    dve.wait_ge(y2_done, n_(l, m) + 1)
                    nc.vector.tensor_tensor(hm, yb[:, mp], hm, ALU.add).then_inc(h_ready, 1)

            with dve.Fori(0, L) as l:
                attention_pipeline(dve, l, attention_step)
                ffn_pipeline(dve, l, ffn_step)
            dve.wait_ge(h_ready, NB * (L + 1) + START)
            for q in range(4):
                x1q = X1[:, 4 * q:4 * q + 4].rearrange("p b d -> p (b d)")
                nc.vector.scalar_tensor_tensor(out=x1q, in0=H[:, 4 * q:4 * q + 4].rearrange("p b d -> p (b d)"),
                                               scalar=tg[:, 1:2], in1=x1q, op0=ALU.mult, op1=ALU.add).then_inc(fin_ready, 1)

        @block.tensor
        def _(pe):
            for s in PE_SEMS + [c_xT, c_qv, c_v, c_sc, c_pT, c_o]:
                pe.sem_inc(s, START)
            pe.wait_ge(in_ready, 16 * N_INPUTS)
            with pe.Fori(0, NB // GB) as g:
                tiles = [slice(128 * j, 128 * j + 128) for j in range(GB)]
                pe.wait_ge(c_xh, g + 1 + START)
                for t in tiles:
                    i = nc.tensor.transpose(A[0][:, t], xh4[:, t], ident[:])
                i.then_inc(c_xT, 1)
                pe.wait_ge(c_ctx, g + 1 + START)
                nc.tensor.matmul(C[1][:], wvT[:], cT, start=True, stop=True)
                for t in tiles:
                    i = nc.tensor.matmul(B[0][:, t], cT[:, t], wvT[:], start=True, stop=True)
                i.then_inc(c_v, 1)
                pe.wait_ge(c_xTs, g + 1 + START)
                nc.tensor.matmul(C[0][:], wqT[:], xhT4, start=True, stop=True).then_inc(c_qv, 1)
                pe.wait_ge(c_qvs, g + 1 + START)
                for t in tiles:
                    i = nc.tensor.matmul(B[1][:, t], qT4[:, t], vT4[:, t], start=True, stop=True)
                i.then_inc(c_sc, 1)
                pe.wait_ge(c_exp, g + 1 + START)
                for t in tiles:
                    i = nc.tensor.transpose(A[0][:, t], p4[:, t], ident[:])
                i.then_inc(c_pT, 1)
                pe.wait_ge(c_vs, g + 1 + START)
                pe.wait_ge(c_pTs, g + 1 + START)
                for t in tiles:
                    i = nc.tensor.matmul(A[1][:, t], pT4[:, t], v4[:, t], start=True, stop=True)
                i.then_inc(c_o, 1)
            pe.wait_ge(h_ready, NB + START)
            pe.wait_ge(consts_act, 2)

            def weights(l, at, size, rows=128):
                return WB[0:rows, ds((l & 1) * W_SIZE + at, size)]

            def attention_step(l, it, par, project, attend, finish):
                n, a, m = it, it - 1, it - 2

                def chunk(c):
                    pe.wait_ge(A_out, a_at(l, n, c) - 1)
                    nc.tensor.matmul(A[c % 2][:], xsT[:, par], weights(l, CHUNK_AT[c], 512), start=True,
                                     stop=True).then_inc(A_full, 1)

                def turn_qk(g):
                    pe.wait_ge(qk_ready, nk(l, a, 4, g) + 1)
                    pe.wait_ge(B_out, b_at(l, a, g) - 1)
                    for t in range(4):
                        i = nc.tensor.transpose(B[g % 2][:, 128 * t:128 * t + 128], u[:, 1 - par, g, 128 * t:128 * t + 128],
                                                ident[:])
                    i.then_inc(B_full, 1)

                def scores(s):
                    pe.wait_ge(B_out, b_at(l, a, 2 * s + 2))
                    pe.wait_ge(C_out, c_at(l, a, 2 * s))
                    for e in range(2):
                        nc.tensor.matmul(C[e][:].rearrange("p (h k) -> p h k", h=4), identb[:],
                                         maskb[:].unsqueeze(1).broadcast_to([128, 4, 128]), start=True, stop=False,
                                         skip_group_check=True)
                    for t in range(4):
                        for e in range(2):
                            r = slice(64 * e, 64 * e + 64)
                            i = nc.tensor.matmul(C[e][:, 128 * t:128 * t + 128], qkT[r, 2 * s, t], qkT[r, 2 * s + 1, t],
                                                 start=False, stop=(t == 3), skip_group_check=True)
                            if t == 3:
                                i.then_inc(C_full, 1)

                def turn_p(g):
                    pe.wait_ge(P_ready, nk(l, a, 4, g) + 1)
                    pe.wait_ge(B_out, b_at(l, a, 4 + g) - 1)
                    for t in range(4):
                        i = nc.tensor.transpose(B[g % 2][:, 128 * t:128 * t + 128], P[:, g, t], ident[:])
                    i.then_inc(B_full, 1)

                def values(g):
                    s, e = g // 2, g % 2
                    pe.wait_ge(B_out, b_at(l, a, 4 + g) + 1)
                    pe.wait_ge(A_out, a_at(l, a, 6))
                    pe.wait_ge(D_out, nk(l, a, 2, s))
                    for t in range(4):
                        h = 8 * s + 2 * t + e
                        i = nc.tensor.matmul(Dk[64 * e:64 * e + 64, 128 * t:128 * t + 128], v[:, 1 - par, DH * h:DH * h + DH],
                                             PT[:, e, t], start=True, stop=True)
                    i.then_inc(pv_done, 1)

                if project:
                    pe.wait_ge(xw_ready, n_(l, n) + 1)
                    pe.wait_ge(xhT_ready, n_(l, 0 if isinstance(n, int) else n - 2))
                    nc.tensor.transpose(E[:, 0:S], xw[:, par], ident[:]).then_inc(xT_done, 1)
                if attend:
                    turn_qk(0)
                    turn_qk(1)
                if finish:
                    pe.wait_ge(D_out, nk(l, m, 2, 2))
                    pe.wait_ge(xhT_ready, n_(l, m))
                    if project:
                        pe.wait_ge(xsT_ready, n_(l, n) + 1)
                    for k in range(INNER // 128):
                        i = nc.tensor.matmul(E[:, 0:D], OT[:, par, k // 4, k % 4], weights(l, WO_AT + k * D, D),
                                             start=(k == 0), stop=(k == INNER // 128 - 1))
                    i.then_inc(Wo_done, 1)
                if project:
                    if isinstance(it, int) and it == 0:
                        pe.wait_ge(w_ready, l * 80 + 80)
                    pe.wait_ge(xsT_ready, n_(l, n) + 1)
                    chunk(0)
                if attend:
                    scores(0)
                    turn_qk(2)
                    turn_qk(3)
                if project:
                    chunk(1)
                if finish:
                    pe.wait_ge(res_done, n_(l, m) + 1)
                    nc.tensor.matmul(E[:, 0:64], ident[:], H[:, ds(m, 1), 0:64].rearrange("p o d -> p (o d)"), start=True, stop=True)
                    nc.tensor.matmul(E[:, 64:128], shf[:], H[:, ds(m, 1), 64:128].rearrange("p o d -> p (o d)"), start=True,
                                     stop=True).then_inc(xs_done, 1)
                if attend:
                    scores(1)
                if project:
                    chunk(2)
                if attend:
                    turn_p(0)
                    turn_p(1)
                if project:
                    chunk(3)
                if finish:
                    pe.wait_ge(xh_ready, n_(l, m) + 1)
                    nc.tensor.transpose(E[:, 0:S], xh[:, par], ident[:]).then_inc(xhT_done, 1)
                if attend:
                    if isinstance(it, int) and it == 1:
                        pe.wait_ge(h_ready, n_(l, 0) + NB)
                    values(0)
                    values(1)
                    turn_p(2)
                    turn_p(3)
                if project:
                    chunk(4)
                if attend:
                    values(2)
                    values(3)
                if project:
                    chunk(5)

            def ffn_step(l, it, par, up, down):
                if up:
                    n = it
                    X, full, free = (A, A_full, A_out) if par == 0 else (C, C_full, C_out)
                    pe.wait_ge(xf_ready, n_(l, n) + 1)
                    for j in range(2):
                        pe.wait_ge(free, ffn_at(l, n, par, j) - 1)
                        i = nc.tensor.matmul(X[j][:, 0:DI], xf[:, par], weights(l, W1_AT + (DI if j == 0 else 0), DI),
                                             start=True, stop=True)
                        i.then_inc(full, 1)
                if down:
                    m, mp = it - 1, 1 - par
                    at = l * B_PER + NB * 8 + m + START
                    pe.wait_ge(hh_ready, n_(l, m) + 1)
                    pe.wait_ge(B_out, at - 1)
                    for t in range(KT2):
                        w = min(128, DI - 128 * t)
                        i = nc.tensor.transpose(B[mp][0:w, 128 * t:128 * t + 128], hh[:, mp, 128 * t:128 * t + w], ident[:])
                    i.then_inc(B_full, 1)
                    pe.wait_ge(B_out, at + 1)
                    pe.wait_ge(h_ready, n_(l, m) + NB)
                    pe.wait_ge(D_out, n_(l, 0) + l * NB + 2 * NB)
                    for t in range(KT2):
                        w = min(128, DI - 128 * t)
                        i = nc.tensor.matmul(Dk[:, 0:D], hT[0:w, mp, t], weights(l, W2_AT + t * D, D, w), start=(t == 0),
                                             stop=(t == KT2 - 1))
                    i.then_inc(y_done, 1)

            with pe.Fori(0, L) as l:
                attention_pipeline(pe, l, attention_step)
                ffn_pipeline(pe, l, ffn_step)


def rotary_constants():
    f = np.float32
    half = np.arange(0, DH, 2, dtype=f)
    inv_freq = (f(1.0) / f(10000.0) ** (half / f(DH))).astype(f)
    t = np.arange(S, dtype=f)
    freqs = t[:, None] * inv_freq[None, :]
    base = ((half + f(0.4 * DH)) / f(1.4 * DH)).astype(f)
    power = ((t - S // 2) / f(WINDOW // 2)).astype(f)
    scale = (base[None, :] ** power[:, None]).astype(f)
    cos, sin = np.cos(freqs), np.sin(freqs)
    q = np.stack([np.concatenate([cos * scale * f(8)] * 2, -1), np.concatenate([cos / scale] * 2, -1)], 1)
    s = np.stack([np.concatenate([-sin * scale * f(8), sin * scale * f(8)], -1),
                  np.concatenate([-sin / scale, sin / scale], -1)], 1)
    return q.astype(f), s.astype(f)


def band_mask():
    i, j = np.arange(S)[:, None], np.arange(S)[None, :]
    return np.where((i < j) | (i > j + WINDOW), NEG, 0.0).astype(np.float32)


_INS = ['x', 'ctx_1024', 'g_xattn', 'g_ffn', 'L0_xattn_Wq', 'L0_xattn_bq', 'L0_xattn_qk_b', 'L0_xattn_Wv',
        'L0_xattn_bv', 'L0_ffn_Wqkv', 'L0_ffn_q_scale', 'L0_ffn_k_scale', 'L0_ffn_Wo', 'L0_ffn_ln_g', 'L0_ffn_ln_b',
        'L0_ffn_W1', 'L0_ffn_b1', 'L0_ffn_W2', 'L0_ffn_b2']

_TRANSPOSED = ('ctx_1024', 'L0_xattn_Wq', 'L0_xattn_Wv', 'L0_ffn_ln_g', 'L0_ffn_ln_b')


def kernel(**inputs):
    import concourse.bacc as _bacc
    from concourse.bass_utils import run_bass_kernel_spmd as _run

    nc = _bacc.Bacc("TRN2", target_bir_lowering=False, num_devices=1)
    arrays, args = {}, []
    cos, sin = rotary_constants()
    consts = {"rot_cos": cos, "rot_sin": sin, "band": band_mask(), "eye": np.eye(128, dtype=np.float32),
              "shift": np.eye(128, k=1, dtype=np.float32)}
    for name in _INS + list(consts):
        a = np.asarray(consts[name] if name in consts else inputs[name])
        if name in _TRANSPOSED:
            a = a.swapaxes(-1, -2)
        a = np.ascontiguousarray(a)
        arrays[f"in_{name}_dram"] = a
        args.append(nc.dram_tensor(f"in_{name}_dram", a.shape, mybir.dt.from_np(a.dtype), kind="ExternalInput").ap())
    out = nc.dram_tensor("out_dram", (NB, S, D), mybir.dt.float32, kind="ExternalOutput").ap()
    program(nc, *args, out)
    return _run(nc, [arrays], core_ids=[0]).results[0]["out_dram"]
```

```python
import numpy as np
import concourse.bass as bass
from concourse import mybir
from contextlib import ExitStack

L, NB, S, D = 6, 16, 128, 128
N = L * NB
HEADS, DH, WINDOW = 16, 64, 32
INNER = HEADS * DH
DI = int(D * 4 * 2 / 3)
HC = 512 // DH
NCH = 2 * INNER // 512
CHUNK_AT = [0, INNER, 512, INNER + 512, 2 * INNER, 2 * INNER + 512]
QKV = 3 * INNER
BLOCK = QKV // (NB // 2)
WO_AT = 0
W1_AT = WO_AT + (INNER // 128) * D
W2_AT = W1_AT + 2 * DI
KT2 = -(-DI // 128)
B1_AT = W2_AT + KT2 * D
B2_AT = B1_AT + 2 * DI
W_SIZE = B2_AT + D
LOADS = 6
START = 16
GB = 4
CROSS_HEADS = 16
NEG = -1e30
SS_SCALE_LOG2 = 20


def program(nc, x, ctxT, g_xattn, g_ffn, Wq, bq, qk_b, Wv, bv, Wqkv, q_scale, k_scale, Wo, ln_g, ln_b, W1, b1, W2,
            b2, rot_cos, rot_sin, band, eye, shift, out):
    F32, F32R, BF16 = mybir.dt.float32, mybir.dt.float32r, mybir.dt.bfloat16
    ALU, ACT, AX = mybir.AluOpType, mybir.ActivationFunctionType, mybir.AxisListType.X
    ds = bass.ds
    es = ExitStack()

    def sb(name, shape, dt=F32):
        return es.enter_context(nc.sbuf_tensor(name, shape, dt))

    def sem(name):
        return es.enter_context(nc.semaphore(name))

    with es:
        H = sb("H", [128, NB, D])
        X1 = sb("X1", [128, NB, D])
        Wraw = sb("Wraw", [128, QKV])
        Wh = sb("Wh", [128, 2 * QKV], F32R)
        Wl = sb("Wl", [128, 2 * QKV], F32R)
        WB = sb("WB", [128, 2 * W_SIZE])
        TC = sb("TC", [128, L, 2, DH])
        TS = sb("TS", [128, L, 2, DH])
        rc = sb("rc", [128, 2, DH])
        rsn = sb("rsn", [128, 2, DH])
        qs = sb("qs", [128, 2, L, DH])
        ident = sb("ident", [128, 128])
        shf = sb("shf", [128, 128])
        identb = sb("identb", [128, 128], BF16)
        maskf = sb("maskf", [128, 128])
        maskb = sb("maskb", [128, 128], BF16)
        gate2 = sb("gate2", [128, 2])
        tg = sb("tg", [128, 2])
        lng = sb("lng", [128, L])
        lnb = sb("lnb", [128, L])
        wqT = sb("wqT", [128, 128])
        wvT = sb("wvT", [128, 128])
        bqc = sb("bqc", [128, 3])
        bqs = sb("bqs", [128, 1])
        bvb = sb("bvb", [128, 128])
        xw = sb("xw", [128, 2, D])
        xsh = sb("xsh", [128, 2, S], F32R)
        xsl = sb("xsl", [128, 2, S], F32R)
        sq = sb("sq", [128, 2, 512])
        ss = sb("ss", [128, 2, 4 * HC])
        ssc = sb("ssc", [128, 2, 4 * HC])
        lnv = sb("lnv", [128, 2, 4 * HC])
        rn = sb("rn", [128, 2, 4 * HC])
        u = sb("u", [128, 2, NCH, 512])
        t2 = sb("t2", [128, 2, 512])
        qkT = sb("qkT", [128, NCH, 4, 128])
        nm = sb("nm", [128, 16])
        rs = sb("rs", [128, 16])
        P = sb("P", [128, 2, 4, 4, 128])
        PT = sb("PT", [128, 2, 4, 128])
        v = sb("v", [128, 2, HEADS, DH + 1])
        O = sb("O", [128, INNER])
        raw = sb("raw", [128, 2, 512])
        OT = sb("OT", [128, 2, 4, 128])
        bst = sb("bst", [128, 2, 6])
        mv = sb("mv", [128, 2, 2])
        lv = sb("lv", [128, 2])
        rstd = sb("rstd", [128, 2])
        xh = sb("xh", [128, 2, D])
        xf = sb("xf", [128, S])
        gate = sb("gate", [128, DI])
        value = sb("value", [128, DI])
        hh = sb("hh", [128, DI])
        hT = sb("hT", [128, KT2, 128])
        yb = sb("yb", [128, D])
        cT = t2[:, 0, :]
        xh4, xhT4, qT4, vT4 = (u[:, 0, j, :] for j in range(4))
        p4, pT4, v4, out4 = (u[:, 1, j, :] for j in range(4))
        ctxS = P[:, 0].rearrange("p g h k -> p (g h) k")
        st4 = sb("st4", [128, GB, 6])
        mv4 = sb("mv4", [128, GB, 2])
        lv4 = sb("lv4", [128, GB])
        rstd4 = sb("rstd4", [128, GB])
        mx4 = sb("mx4", [128, GB])
        nm4 = sb("nm4", [128, GB])
        sum4 = sb("sum4", [128, GB])
        rc4 = sb("rc4", [128, GB])
        rg4 = sb("rg4", [128, GB])
        cols = sb("cols", [128, 2])
        eps_col, exp_col = cols[:, 0:1], cols[:, 1:2]

        def bank(name):
            return es.enter_context(nc.psum_tensor("bank_" + name, [128, 512], F32))

        A = [bank("A0"), bank("A1")]
        B = [bank("B0"), bank("B1")]
        C = [bank("C0"), bank("C1")]
        Dk = bank("D")
        E = bank("E")

        in_ready, raw_loaded, w_ready, out_done = (sem(s) for s in ("in_ready", "raw_loaded", "w_ready", "out_done"))
        ch_full = sem("ch_full")
        v_full = sem("v_full")
        qkT_full = sem("qkT_full")
        sc_full = sem("sc_full")
        PT_full = sem("PT_full")
        pv_full = sem("pv_full")
        OT_full = sem("OT_full")
        Wo_full = sem("Wo_full")
        xT_full = sem("xT_full")
        xs_full = sem("xs_full")
        xhT_full = sem("xhT_full")
        gv_full = sem("gv_full")
        hT_full = sem("hT_full")
        y_full = sem("y_full")
        PE_SEMS = [ch_full, v_full, qkT_full, sc_full, PT_full, pv_full, OT_full, Wo_full, xT_full, xs_full, xhT_full,
                   gv_full, hT_full, y_full]
        rot_done = sem("rot_done")
        ss_done = sem("ss_done")
        ss_ready = sem("ss_ready")
        mx_done = sem("mx_done")
        sc_out = sem("sc_out")
        rs_done = sem("rs_done")
        pv_out = sem("pv_out")
        res_done = sem("res_done")
        bst_done = sem("bst_done")
        mv_ready = sem("mv_ready")
        xh_ready = sem("xh_ready")
        xf_ready = sem("xf_ready")
        gv_out = sem("gv_out")
        hh_ready = sem("hh_ready")
        y_out = sem("y_out")
        xs_split = sem("xs_split")
        high_done = sem("high_done")
        W_split = sem("W_split")
        h_ready = sem("h_ready")
        DVE_SEMS = [rot_done, ss_done, ss_ready, mx_done, sc_out, rs_done, pv_out, res_done, bst_done, mv_ready,
                    xh_ready, xf_ready, gv_out, hh_ready, y_out, xs_split, high_done, W_split, h_ready]
        xsh_ready = sem("xsh_ready")
        sq_done = sem("sq_done")
        raw_ready = sem("raw_ready")
        v_ready = sem("v_ready")
        qkT_ready = sem("qkT_ready")
        exp_done = sem("exp_done")
        PT_ready = sem("PT_ready")
        OT_ready = sem("OT_ready")
        ln_done = sem("ln_done")
        rn_ready = sem("rn_ready")
        lv_done = sem("lv_done")
        rstd_ready = sem("rstd_ready")
        gelu_done = sem("gelu_done")
        hT_ready = sem("hT_ready")
        ACT_SEMS = [xsh_ready, sq_done, raw_ready, v_ready, qkT_ready, exp_done, PT_ready, OT_ready, ln_done, rn_ready,
                    lv_done, rstd_ready, gelu_done, hT_ready]
        xw_ready = sem("xw_ready")
        t2_done = sem("t2_done")
        add_done = sem("add_done")
        qk_ready = sem("qk_ready")
        POOL_SEMS = [xw_ready, t2_done, add_done, qk_ready]
        tables_ready, tanh_done, consts_done = sem("tables_ready"), sem("tanh_done"), sem("consts_done")
        bqs_ready, consts_act = sem("bqs_ready"), sem("consts_act")
        c_st, c_mv, c_lv, c_rstd, c_xh, c_ctx = (sem(s) for s in ("c_st", "c_mv", "c_lv", "c_rstd", "c_xh", "c_ctx"))
        c_xT, c_xTs, c_qv, c_v, c_qvs, c_vs = (sem(s) for s in ("c_xT", "c_xTs", "c_qv", "c_v", "c_qvs", "c_vs"))
        c_sc, c_mx, c_nm, c_exp, c_rc, c_rg, c_pT, c_pTs, c_o, c_x1 = (
            sem(s) for s in ("c_sc", "c_mx", "c_nm", "c_exp", "c_rc", "c_rg", "c_pT", "c_pTs", "c_o", "c_x1"))
        fin_ready = sem("fin_ready")
        wait_met = sem("wait_met")

        def n_(n):
            return n + START

        def nk(n, per, k):
            return n * per + k + START

        def pipeline(eng, step):
            last = N - NB + 1

            def peeled(it):
                step(it, it % 2, *[0 <= it - lag < N for lag in (0, 1, 2, 3, 4, -1)], it % 2 == 1 and 1 <= it < last)

            for it in range(-1, 5):
                peeled(it)
            with eng.Fori(0, (last - 5) // 2) as pair:
                step(pair * 2 + 5, 1, True, True, True, True, True, True, True)
                step(pair * 2 + 6, 0, True, True, True, True, True, True, False)
            with eng.Fori(0, (N - 1 - last) // 2) as pair:
                step(pair * 2 + last, 1, True, True, True, True, True, True, False)
                step(pair * 2 + last + 1, 0, True, True, True, True, True, True, False)
            for it in range(N - 1, N + 4):
                peeled(it)

        USERS = {"chunk": (0, 4, rot_done), "up": (4, 2, gv_out), "v": (1, 2, v_ready),
                 "turn_o": (3, 2, OT_ready), ("turn_o", 0): (2, 2, OT_ready), "turn_p": (2, 4, PT_ready), "turn_qk": (1, 4, qkT_ready),
                 "turn_h": (4, 1, hT_ready),
                 "Wo": (3, 1, res_done), "xs": (3, 1, xh_ready), "xhT": (3, 1, xf_ready), "xT": (-1, 1, xs_split),
                 "down": (4, 1, y_out)}
        BANK_USERS = [
            (A[0], [("chunk", 0), ("up", 0), ("v", 0), ("chunk", 2)]),
            (A[1], [("chunk", 1), ("up", 1), ("v", 1), ("chunk", 3)]),
            (B[0], [("turn_qk", 0), ("turn_qk", 1), ("turn_qk", 2), ("turn_p", 2), ("turn_h", 0), ("turn_o", 0)]),
            (B[1], [("turn_p", 0), ("turn_o", 1), ("turn_p", 1), ("turn_qk", 3), ("turn_p", 3)]),
            (E, [("Wo", 0), ("xs", 0), ("xhT", 0), ("xT", 0), ("down", 0)])]

        def bank_of(kind, k):
            return next(b for b, users in BANK_USERS if (kind, k) in users)

        def bank_left(it, kind, k=0):
            users = next(users for _, users in BANK_USERS if (kind, k) in users)
            place = users.index((kind, k))
            for back in range(1, 4 * len(users)):
                turns, at = divmod(place - back, len(users))
                other, ok = users[at]
                lag, per, counter = USERS.get(users[at], USERS[other])
                n = it + turns - lag
                if not isinstance(it, int) or 0 <= n < N:
                    return counter, nk(n, per, ok) + 1
            return USERS[kind][2], START

        def weights(n, at, size, rows=128):
            return WB[0:rows, ds(((n // NB) % 2) * W_SIZE + at, size)]

        def layer(n):
            return ds(n // NB, 1)

        def row_of(t, n):
            return t[:, ds(n % NB, 1)].rearrange("p o d -> p (o d)")

        def halves(ap):
            return ap.rearrange("p (h a d) -> p h a d", h=HC, a=2)

        def by_head(ap, n=HC):
            return ap.rearrange("p (h d) -> p h d", h=n)

        def spread(ap, n, m):
            return ap.unsqueeze(2).broadcast_to([128, n, m])

        N_SMALL = 17
        N_INPUTS = N_SMALL + 2
        block = es.enter_context(nc.Block())

        @block.sync
        def _(sp):
            sp.dma_start(H[:], x.rearrange("b s d -> s b d")).then_inc(in_ready, 16)
            sp.dma_start(ctxS[:], ctxT.rearrange("b d s -> d b s")).then_inc(in_ready, 16)
            small = [
                (ident[:], eye), (shf[:], shift), (maskf[:], band), (rc[:], rot_cos), (rsn[:], rot_sin),
                (wqT[:], Wq), (wvT[:], Wv),
                (bqc[:, 0:1], bq.rearrange("(p o) -> p o", o=1)), (bqc[:, 1:2], qk_b.rearrange("(p o) -> p o", o=1)),
                (bqc[:, 2:3], bv.rearrange("(p o) -> p o", o=1)),
                (bvb[:], bv.partition_broadcast(128)),
                (gate2[:, 0:1], g_xattn.partition_broadcast(128)), (gate2[:, 1:2], g_ffn.partition_broadcast(128)),
                (qs[:, 0], q_scale.partition_broadcast(128)), (qs[:, 1], k_scale.partition_broadcast(128)),
                (lng[:], ln_g), (lnb[:], ln_b),
            ]
            assert len(small) == N_SMALL
            for dst, src in small:
                sp.dma_start(dst, src).then_inc(in_ready, 16)
            for l in range(L):
                if l >= 1:
                    sp.wait_ge(W_split, NB // 2 * l + START)
                sp.dma_start(Wraw[:], Wqkv[l]).then_inc(raw_loaded, 16)
                if l >= 1:
                    sp.wait_ge(w_ready, 16 * LOADS * l)
                if l >= 2:
                    sp.wait_ge(h_ready, NB * l + START)
                o = (l % 2) * W_SIZE
                sp.dma_start(WB[:, o + WO_AT:o + W1_AT].rearrange("p (k n) -> p k n", n=D),
                             Wo[l].rearrange("(k p) n -> p k n", p=128)).then_inc(w_ready, 16)
                sp.dma_start(WB[:, o + W1_AT:o + W2_AT], W1[l]).then_inc(w_ready, 16)
                sp.dma_start(WB[:, o + W2_AT:o + W2_AT + (KT2 - 1) * D].rearrange("p (k n) -> p k n", n=D),
                             W2[l, 0:(KT2 - 1) * 128].rearrange("(k p) n -> p k n", p=128)).then_inc(w_ready, 16)
                sp.dma_start(WB[0:DI - (KT2 - 1) * 128, o + W2_AT + (KT2 - 1) * D:o + B1_AT],
                             W2[l, (KT2 - 1) * 128:DI]).then_inc(w_ready, 16)
                sp.dma_start(WB[:, o + B1_AT:o + B2_AT], b1[l].partition_broadcast(128)).then_inc(w_ready, 16)
                sp.dma_start(WB[:, o + B2_AT:o + W_SIZE], b2[l].partition_broadcast(128)).then_inc(w_ready, 16)
            for q in range(4):
                sp.wait_ge(fin_ready, q + 1)
                sp.dma_start(out[4 * q:4 * q + 4].rearrange("b s d -> s b d"),
                             X1[:, 4 * q:4 * q + 4]).then_inc(out_done, 16)
            sp.wait_ge(out_done, 64)

        @block.gpsimd
        def _(pool):
            for s in POOL_SEMS:
                pool.sem_inc(s, START)

            def step(it, par, project, score, weigh, finish, feed, ahead, split):
                n = it

                def rotate(c):
                    w = c % 2
                    pool.wait_ge(raw_ready, nk(n, 4, c) + 1)
                    pool.sem_inc(wait_met, 1)
                    nc.gpsimd.tensor_tensor(halves(t2[:, w]), halves(raw[:, w])[:, :, ::-1, :],
                                            TS[:, layer(n), w].broadcast_to([128, HC, DH]).rearrange(
                                                "p h (a d) -> p h a d", a=2), ALU.mult).then_inc(t2_done, 1)
                    pool.wait_ge(t2_done, nk(n, 4, c) + 1)
                    pool.wait_ge(rot_done, nk(n, 4, c) + 1)
                    nc.gpsimd.tensor_tensor(u[:, par, c], u[:, par, c], t2[:, w], ALU.add).then_inc(add_done, 1)

                def normalise(half):
                    pool.wait_ge(rn_ready, nk(n, 2, half) + 1)
                    for c in (2 * half, 2 * half + 1):
                        pool.wait_ge(add_done, nk(n, 4, c) + 1)
                        nc.gpsimd.tensor_tensor(by_head(u[:, par, c]), by_head(u[:, par, c]),
                                                spread(rn[:, par, HC * c:HC * c + HC], HC, DH),
                                                ALU.mult).then_inc(qk_ready, 1)

                if project:
                    rotate(0)
                    rotate(1)
                    normalise(0)
                if ahead:
                    pool.wait_ge(h_ready, n_(it + 1) + 1)
                    pool.wait_ge(xT_full, n_(it + 1) - 1)
                    pool.sem_inc(wait_met, 1)
                    nc.gpsimd.tensor_copy(xw[:, 1 - par], row_of(H, it + 1)).then_inc(xw_ready, 1)
                if project:
                    rotate(2)
                    rotate(3)
                    normalise(1)

            pool.wait_ge(in_ready, 16 * N_INPUTS)
            pool.sem_inc(c_ctx, START)
            with pool.Fori(0, NB // GB) as g:
                pool.wait_ge(c_v, g + START)
                pool.sem_inc(wait_met, 1)
                nc.gpsimd.tensor_copy(cT, ctxS[:, ds(g * GB, GB)].rearrange("p b d -> p (b d)")).then_inc(c_ctx, 1)
            pipeline(pool, step)

        @block.scalar
        def _(act):
            for s in ACT_SEMS + [c_lv, c_rstd, c_xTs, c_qvs, c_exp, c_pTs]:
                act.sem_inc(s, START)
            act.wait_ge(in_ready, 16 * N_INPUTS)
            nc.scalar.activation(tg[:], gate2[:], ACT.Tanh).then_inc(tanh_done, 1)
            nc.scalar.copy(identb[:], ident[:]).then_inc(consts_act, 1)
            nc.scalar.copy(maskb[:], maskf[:]).then_inc(consts_act, 1)
            nc.scalar.preload_act_table_set("natural_log_exp_and_others")

            def cross_rstd(k):
                act.wait_ge(c_mv, k + 1)
                nc.scalar.activation(lv4[:], mv4[:, :, 1], ACT.Ln, bias=eps_col).then_inc(c_lv, 1)
                act.wait_ge(c_lv, k + 1)
                nc.scalar.activation(rstd4[:], lv4[:], ACT.Exp, scale=-0.5).then_inc(c_rstd, 1)

            act.wait_ge(consts_done, 1)
            act.wait_ge(bqs_ready, 1)
            with act.Fori(0, NB // GB) as g:
                cross_rstd(g * 2 + START)
                act.wait_ge(c_xT, g + 1 + START)
                nc.scalar.copy(xhT4, A[0][:]).then_inc(c_xTs, 1)
                act.wait_ge(c_qv, g + 1 + START)
                nc.scalar.activation(qT4, C[0][:], ACT.Identity, bias=bqs[:])
                nc.scalar.activation(vT4, C[1][:], ACT.Identity, bias=bqc[:, 2:3]).then_inc(c_qvs, 1)
                act.wait_ge(c_nm, g + 1 + START)
                for j in range(GB):
                    i = nc.scalar.activation(p4[:, 128 * j:128 * j + 128], B[1][:, 128 * j:128 * j + 128], ACT.Exp,
                                             bias=nm4[:, j:j + 1], scale=(D / CROSS_HEADS) ** -0.5,
                                             accum_out=sum4[:, j:j + 1])
                i.then_inc(c_exp, 1)
                act.wait_ge(c_pT, g + 1 + START)
                nc.scalar.copy(pT4, A[0][:]).then_inc(c_pTs, 1)
                cross_rstd(g * 2 + 1 + START)

            def step(it, par, project, score, weigh, finish, feed, ahead, split):
                n, a, c_, m, f = (it - k for k in range(5))

                def square_and_copy(c):
                    act.wait_ge(ch_full, nk(n, 4, c) + 1)
                    act.wait_ge(ss_done, nk(n, 4, c) - 1)
                    nc.scalar.activation(sq[:, c % 2], A[c % 2][:], ACT.Square).then_inc(sq_done, 1)
                    act.wait_ge(t2_done, nk(n, 4, c) - 1)
                    nc.scalar.copy(raw[:, c % 2], A[c % 2][:]).then_inc(raw_ready, 1)

                def norms(half):
                    b, p = (n, par) if half == 0 else (a, 1 - par)
                    w = slice(2 * HC * half, 2 * HC * half + 2 * HC)
                    act.wait_ge(ss_ready, nk(b, 2, half) + 1)
                    nc.scalar.activation(lnv[:, p, w], ssc[:, p, w], ACT.Ln,
                                         scale=float(2 ** SS_SCALE_LOG2)).then_inc(ln_done, 1)
                    act.wait_ge(ln_done, nk(b, 2, half) + 1)
                    act.wait_ge(qk_ready, nk(b, 4, 2 * half - 6))
                    nc.scalar.activation(rn[:, p, w], lnv[:, p, w], ACT.Exp, scale=-0.5,
                                         bias=exp_col).then_inc(rn_ready, 1)

                def v_out(j):
                    act.wait_ge(v_full, nk(a, 2, j) + 1)
                    act.wait_ge(pv_full, nk(a, 4, -4))
                    nc.scalar.copy(v[:, 1 - par, HC * j:HC * j + HC, 0:DH], by_head(A[j][:])).then_inc(v_ready, 1)

                def qk_out(g):
                    act.wait_ge(qkT_full, nk(a, 4, g) + 1)
                    act.wait_ge(sc_full, nk(a, 4, -2 if g < 2 else 0))
                    nc.scalar.copy(qkT[:, g].rearrange("p t n -> p (t n)"), bank_of("turn_qk", g)[:]).then_inc(qkT_ready, 1)

                def exp(g):
                    b, p = (a, 1 - par) if g < 2 else (c_, par)
                    act.wait_ge(sc_out, nk(b, 4, g) + 1)
                    pg = P[:, p, g].rearrange("p h k -> p (h k)")
                    nc.scalar.activation(pg, pg, ACT.Exp).then_inc(exp_done, 1)

                def p_out(g):
                    act.wait_ge(PT_full, nk(c_, 4, g) + 1)
                    act.wait_ge(pv_full, nk(c_, 4, g) - 1)
                    nc.scalar.copy(PT[:, g % 2].rearrange("p h k -> p (h k)"),
                                   bank_of("turn_p", g)[:]).then_inc(PT_ready, 1)

                def o_out(s):
                    b = (c_, m)[s]
                    act.wait_ge(OT_full, nk(b, 2, s) + 1)
                    act.wait_ge(Wo_full, n_(b))
                    nc.scalar.copy(OT[:, s].rearrange("p t n -> p (t n)"), bank_of("turn_o", s)[:]).then_inc(OT_ready, 1)

                def gelu():
                    act.wait_ge(gv_out, nk(f, 2, 0) + 1)
                    nc.scalar.activation(gate[:], gate[:], ACT.Gelu).then_inc(gelu_done, 1)

                def h_out():
                    act.wait_ge(hT_full, n_(f) + 1)
                    act.wait_ge(y_full, n_(f))
                    nc.scalar.copy(hT[:, 0:KT2 - 1].rearrange("p t n -> p (t n)"),
                                   bank_of("turn_h", 0)[:, 0:(KT2 - 1) * 128])
                    nc.scalar.copy(hT[0:DI - (KT2 - 1) * 128, KT2 - 1],
                                   bank_of("turn_h", 0)[0:DI - (KT2 - 1) * 128,
                                                        (KT2 - 1) * 128:KT2 * 128]).then_inc(hT_ready, 1)

                if weigh:
                    p_out(0)
                if score:
                    qk_out(0)
                if finish:
                    o_out(1)
                if score:
                    qk_out(1)
                if project:
                    square_and_copy(0)
                if score:
                    norms(1)
                if weigh:
                    exp(2)
                    exp(3)
                if feed:
                    nc.scalar.preload_act_table(ACT.Gelu)
                    gelu()
                if project:
                    square_and_copy(1)
                if feed:
                    nc.scalar.preload_act_table_set("natural_log_exp_and_others")
                if weigh:
                    p_out(1)
                if project:
                    norms(0)
                if score:
                    v_out(0)
                    qk_out(2)
                if score:
                    qk_out(3)
                if finish:
                    act.wait_ge(mv_ready, n_(m) + 1)
                    nc.scalar.activation(lv[:, par:par + 1], mv[:, par, 1:2], ACT.Ln, bias=eps_col).then_inc(lv_done, 1)
                    act.wait_ge(lv_done, n_(m) + 1)
                    act.wait_ge(xh_ready, n_(m) - 1)
                    nc.scalar.activation(rstd[:, par:par + 1], lv[:, par:par + 1], ACT.Exp,
                                         scale=-0.5).then_inc(rstd_ready, 1)
                if score:
                    v_out(1)
                if weigh:
                    p_out(2)
                    p_out(3)
                if score:
                    exp(0)
                    exp(1)
                if project:
                    square_and_copy(2)
                if feed:
                    h_out()
                if ahead:
                    act.wait_ge(xT_full, n_(it + 1) + 1)
                    act.wait_ge(ch_full, nk(it + 1, 4, -4))
                    act.wait_ge(v_full, nk(it + 1, 2, -2))
                    nc.scalar.copy(xsh[0:64, 1 - par], E[0:64, 0:S])
                    nc.scalar.copy(xsh[64:128, 1 - par, 1:S], E[64:128, 0:S - 1]).then_inc(xsh_ready, 1)
                if project:
                    square_and_copy(3)
                if weigh:
                    o_out(0)

            pipeline(act, step)

        @block.vector
        def _(dve):
            for s in DVE_SEMS + [c_st, c_mv, c_xh, c_vs, c_mx, c_nm, c_rc, c_rg, c_x1]:
                dve.sem_inc(s, START)
            nc.vector.memset(eps_col, 1e-5)
            nc.vector.memset(exp_col, 0.5 * SS_SCALE_LOG2 * float(np.log(2.0)))
            nc.vector.memset(v[:, :, :, DH:DH + 1], 1.0)
            nc.vector.memset(xsh[64:128, :, 0:1].bitcast(F32), 0.0)
            nc.vector.memset(xsl[64:128, :, 0:1].bitcast(F32), 0.0).then_inc(consts_done, 1)
            dve.wait_ge(in_ready, 16 * N_INPUTS)
            nc.vector.tensor_tensor(bqs[:], bqc[:, 0:1], bqc[:, 1:2], ALU.add).then_inc(bqs_ready, 1)
            for w in range(2):
                nc.vector.tensor_tensor(TC[:, :, w], qs[:, w], rc[:, w].unsqueeze(1).broadcast_to([128, L, DH]), ALU.mult)
                for a in range(2):
                    o, i = 32 * a, 32 * (1 - a)
                    nc.vector.tensor_tensor(TS[:, :, w, o:o + 32], qs[:, w, :, i:i + 32],
                                            rsn[:, w, o:o + 32].unsqueeze(1).broadcast_to([128, L, 32]),
                                            ALU.mult).then_inc(tables_ready, 1)

            def group_norm(k, src, dst, done):
                for j in range(GB):
                    i = nc.vector.bn_stats(st4[:, j], src(j))
                i.then_inc(c_st, 1)
                dve.wait_ge(c_st, k + 1)
                dve.sem_inc(wait_met, 1)
                for j in range(GB):
                    i = nc.vector.bn_aggr(mv4[:, j], st4[:, j])
                i.then_inc(c_mv, 1)
                dve.wait_ge(c_rstd, k + 1)
                for j in range(GB):
                    dve.wait_ge(c_mv, k + 1)
                    i = nc.vector.tensor_scalar(dst(j), src(j), mv4[:, j, 0:1], rstd4[:, j:j + 1], ALU.subtract, ALU.mult)
                i.then_inc(done[0], done[1])

            def split_block(k, block):
                part, half = ds(block * BLOCK, BLOCK), ds((k // (NB // 2)) % 2 * QKV + block * BLOCK, BLOCK)
                dve.sem_inc(wait_met, 1)
                nc.vector.tensor_copy(Wh[:, half], Wraw[:, part]).then_inc(high_done, 1)
                dve.wait_ge(high_done, k + 1 + START)
                nc.vector.tensor_tensor(Wl[:, half], Wraw[:, part], Wh[:, half], ALU.subtract).then_inc(W_split, 1)

            with dve.Fori(0, NB // GB) as g:
                def row(t, j):
                    return t[:, ds(g * GB + j, 1)].rearrange("p o d -> p (o d)")
                dve.wait_ge(c_xT, g + START)
                dve.sem_inc(wait_met, 1)
                group_norm(g * 2 + START, lambda j: row(H, j), lambda j: xh4[:, 128 * j:128 * j + 128], (c_xh, 1))
                dve.wait_ge(raw_loaded, 16)
                split_block(g * 2, g * 2)
                split_block(g * 2 + 1, g * 2 + 1)
                dve.wait_ge(c_v, g + 1 + START)
                nc.vector.tensor_tensor(v4.rearrange("p (b d) -> p b d", b=GB), B[0][:].rearrange("p (b d) -> p b d", b=GB),
                                        bvb[:].unsqueeze(1).broadcast_to([128, GB, D]), ALU.add).then_inc(c_vs, 1)
                dve.wait_ge(c_sc, g + 1 + START)
                nc.vector.tensor_reduce(mx4[:], B[1][:].rearrange("p (b d) -> p b d", b=GB), AX, ALU.max).then_inc(c_mx, 1)
                dve.wait_ge(c_mx, g + 1 + START)
                nc.vector.tensor_scalar_mul(nm4[:], mx4[:], -(D / CROSS_HEADS) ** -0.5).then_inc(c_nm, 1)
                dve.wait_ge(c_exp, g + 1 + START)
                nc.vector.reciprocal(rc4[:], sum4[:]).then_inc(c_rc, 1)
                dve.wait_ge(c_rc, g + 1 + START)
                dve.wait_ge(tanh_done, 1)
                nc.vector.tensor_scalar_mul(rg4[:], rc4[:], tg[:, 0:1]).then_inc(c_rg, 1)
                dve.wait_ge(c_rg, g + 1 + START)
                dve.wait_ge(c_o, g + 1 + START)
                for j in range(GB):
                    i = nc.vector.scalar_tensor_tensor(out=row(X1, j), in0=A[1][:, 128 * j:128 * j + 128],
                                                       scalar=rg4[:, j:j + 1], in1=row(H, j), op0=ALU.mult, op1=ALU.add)
                i.then_inc(c_x1, 1)
                dve.wait_ge(c_x1, g + 1 + START)
                dve.sem_inc(wait_met, 1)
                group_norm(g * 2 + 1 + START, lambda j: row(X1, j), lambda j: row(H, j), (h_ready, GB))
            dve.wait_ge(tables_ready, 4)

            def step(it, par, project, score, weigh, finish, feed, ahead, split):
                n, a, c_, m, f = (it - k for k in range(5))

                def rotate(c):
                    w = c % 2
                    dve.wait_ge(sq_done, nk(n, 4, c) + 1)
                    nc.vector.tensor_reduce(ss[:, par, HC * c:HC * c + HC], by_head(sq[:, w]), AX,
                                            ALU.add).then_inc(ss_done, 1)
                    dve.wait_ge(raw_ready, nk(n, 4, c) + 1)
                    dve.wait_ge(qkT_full, nk(n, 4, c) - 7)
                    nc.vector.tensor_tensor(by_head(u[:, par, c]), by_head(A[w][:]),
                                            TC[:, layer(n), w].broadcast_to([128, HC, DH]),
                                            ALU.mult).then_inc(rot_done, 1)

                def bound_norms(half):
                    w = slice(2 * HC * half, 2 * HC * half + 2 * HC)
                    dve.wait_ge(ss_done, nk(n, 4, 2 * half + 2))
                    dve.wait_ge(ln_done, nk(n, 2, half) - 3)
                    nc.vector.tensor_scalar_max(ssc[:, par, w], ss[:, par, w], 1e-24).then_inc(ss_ready, 1)

                def maxima(s):
                    for g in (2 * s, 2 * s + 1):
                        dve.wait_ge(sc_full, nk(a, 4, g) + 1)
                        nc.vector.tensor_reduce(nm[:, 4 * g:4 * g + 4], by_head(C[g % 2][:], 4), AX,
                                                ALU.max).then_inc(mx_done, 1)

                def subtract(s):
                    for g in (2 * s, 2 * s + 1):
                        dve.wait_ge(mx_done, nk(a, 4, g) + 1)
                        dve.wait_ge(PT_full, nk(a, 4, g) - 7)
                        nc.vector.tensor_tensor(P[:, 1 - par, g], by_head(C[g % 2][:], 4),
                                                spread(nm[:, 4 * g:4 * g + 4], 4, 128), ALU.subtract).then_inc(sc_out, 1)

                def split_xs():
                    dve.wait_ge(xsh_ready, n_(it + 1) + 1)
                    nc.vector.tensor_tensor(xsl[0:64, 1 - par], E[0:64, 0:S], xsh[0:64, 1 - par], ALU.subtract)
                    nc.vector.tensor_tensor(xsl[64:128, 1 - par, 1:S], E[64:128, 0:S - 1], xsh[64:128, 1 - par, 1:S],
                                            ALU.subtract).then_inc(xs_split, 1)

                def divide(g):
                    s, e = g // 2, g % 2
                    dve.wait_ge(pv_full, nk(c_, 4, g) + 1)
                    heads = by_head(Dk[:, 0:4 * (DH + 1)], 4)
                    nc.vector.reciprocal(rs[:, 4 * g:4 * g + 4], heads[:, :, DH]).then_inc(rs_done, 1)
                    dve.wait_ge(rs_done, nk(c_, 4, g) + 1)
                    dve.wait_ge(OT_full, nk(c_, 2, s) - 1)
                    nc.vector.tensor_tensor(O[:].rearrange("p (s t e d) -> p s t e d", s=2, t=4, e=2)[:, s, :, e, :],
                                            heads[:, :, 0:DH], spread(rs[:, 4 * g:4 * g + 4], 4, DH),
                                            ALU.mult).then_inc(pv_out, 1)

                def bias(k):
                    dve.wait_ge(gv_full, nk(f, 2, k) + 1)
                    dve.wait_ge(hh_ready, n_(f))
                    nc.vector.tensor_tensor((gate, value)[k][:], A[k][:, 0:DI], weights(f, B1_AT + DI * (1 - k), DI),
                                            ALU.add).then_inc(gv_out, 1)

                if project:
                    rotate(0)
                if weigh:
                    divide(0)
                if feed:
                    bias(0)
                if score:
                    maxima(0)
                if project:
                    rotate(1)
                    bound_norms(0)
                if finish:
                    dve.wait_ge(Wo_full, n_(m) + 1)
                    nc.vector.tensor_tensor(row_of(H, m), E[:, 0:D], row_of(H, m), ALU.add).then_inc(res_done, 1)
                if score:
                    subtract(0)
                if feed:
                    bias(1)
                if feed:
                    dve.wait_ge(gelu_done, n_(f) + 1)
                    dve.wait_ge(gv_out, nk(f, 2, 1) + 1)
                    dve.wait_ge(hT_full, n_(f))
                    nc.vector.tensor_tensor(hh[:], value[:], gate[:], ALU.mult).then_inc(hh_ready, 1)
                if finish:
                    dve.wait_ge(xs_full, n_(m) + 1)
                    nc.vector.bn_stats(bst[:, par], E[:, 0:D]).then_inc(bst_done, 1)
                    dve.wait_ge(bst_done, n_(m) + 1)
                    dve.wait_ge(lv_done, n_(m) - 1)
                    dve.sem_inc(wait_met, 1)
                    nc.vector.bn_aggr(mv[:, par], bst[:, par]).then_inc(mv_ready, 1)
                if weigh:
                    divide(1)
                if finish:
                    dve.wait_ge(rstd_ready, n_(m) + 1)
                    dve.wait_ge(mv_ready, n_(m) + 1)
                    dve.wait_ge(xhT_full, n_(m) - 1)
                    nc.vector.tensor_scalar(xh[:, par], E[:, 0:D], mv[:, par, 0:1], rstd[:, par:par + 1], ALU.subtract,
                                            ALU.mult).then_inc(xh_ready, 1)
                if split:
                    dve.wait_ge(raw_loaded, (it // NB) * 16 + 32)
                    dve.wait_ge(v_full, nk(it - 1, 2, 0))
                    split_block((it - 1) // 2 + NB // 2, (it % NB) // 2)
                if finish:
                    dve.wait_ge(xhT_full, n_(m) + 1)
                    dve.wait_ge(gv_full, nk(m, 2, 0))
                    nc.vector.tensor_scalar(xf[:], E[:, 0:S], lng[:, layer(m)], lnb[:, layer(m)], ALU.mult,
                                            ALU.add).then_inc(xf_ready, 1)
                if project:
                    rotate(2)
                if weigh:
                    divide(2)
                if ahead:
                    split_xs()
                if score:
                    maxima(1)
                    subtract(1)
                if weigh:
                    divide(3)
                if project:
                    rotate(3)
                    bound_norms(1)
                if feed:
                    dve.wait_ge(y_full, n_(f) + 1)
                    nc.vector.tensor_tensor(yb[:], E[:, 0:D], weights(f, B2_AT, D), ALU.add).then_inc(y_out, 1)
                    dve.wait_ge(y_out, n_(f) + 1)
                    nc.vector.tensor_tensor(row_of(H, f), yb[:], row_of(H, f), ALU.add).then_inc(h_ready, 1)

            pipeline(dve, step)
            dve.wait_ge(h_ready, NB * (L + 1) + START)
            for q in range(4):
                x1q = X1[:, 4 * q:4 * q + 4].rearrange("p b d -> p (b d)")
                nc.vector.scalar_tensor_tensor(out=x1q, in0=H[:, 4 * q:4 * q + 4].rearrange("p b d -> p (b d)"),
                                               scalar=tg[:, 1:2], in1=x1q, op0=ALU.mult, op1=ALU.add).then_inc(fin_ready, 1)

        @block.tensor
        def _(pe):
            for s in PE_SEMS + [c_xT, c_qv, c_v, c_sc, c_pT, c_o]:
                pe.sem_inc(s, START)
            pe.wait_ge(in_ready, 16 * N_INPUTS)
            with pe.Fori(0, NB // GB) as g:
                tiles = [slice(128 * j, 128 * j + 128) for j in range(GB)]
                pe.wait_ge(c_xh, g + 1 + START)
                for t in tiles:
                    i = nc.tensor.transpose(A[0][:, t], xh4[:, t], ident[:])
                i.then_inc(c_xT, 1)
                pe.wait_ge(c_ctx, g + 1 + START)
                nc.tensor.matmul(C[1][:], wvT[:], cT, start=True, stop=True)
                for t in tiles:
                    i = nc.tensor.matmul(B[0][:, t], cT[:, t], wvT[:], start=True, stop=True)
                i.then_inc(c_v, 1)
                pe.wait_ge(c_xTs, g + 1 + START)
                nc.tensor.matmul(C[0][:], wqT[:], xhT4, start=True, stop=True).then_inc(c_qv, 1)
                pe.wait_ge(c_qvs, g + 1 + START)
                for t in tiles:
                    i = nc.tensor.matmul(B[1][:, t], qT4[:, t], vT4[:, t], start=True, stop=True)
                i.then_inc(c_sc, 1)
                pe.wait_ge(c_exp, g + 1 + START)
                for t in tiles:
                    i = nc.tensor.transpose(A[0][:, t], p4[:, t], ident[:])
                i.then_inc(c_pT, 1)
                pe.wait_ge(c_vs, g + 1 + START)
                pe.wait_ge(c_pTs, g + 1 + START)
                for t in tiles:
                    i = nc.tensor.matmul(A[1][:, t], pT4[:, t], v4[:, t], start=True, stop=True)
                i.then_inc(c_o, 1)
            pe.wait_ge(h_ready, NB + START)
            pe.wait_ge(consts_act, 2)

            def step(it, par, project, score, weigh, finish, feed, ahead, split):
                n, a, c_, m, f = (it - k for k in range(5))
                def product(bank, p, b, at, done):
                    w = ds((b // NB) % 2 * QKV + at, 512)
                    nc.tensor.matmul(bank[:], xsh[:, p], Wl[:, w], start=True, stop=False)
                    nc.tensor.matmul(bank[:], xsl[:, p], Wh[:, w], start=False, stop=False)
                    nc.tensor.matmul(bank[:], xsh[:, p], Wh[:, w], start=False, stop=True).then_inc(done, 1)

                def chunk(c):
                    pe.wait_ge(*bank_left(it, "chunk", c))
                    product(bank_of("chunk", c), par, n, CHUNK_AT[c], ch_full)

                def v_chunk(j):
                    pe.wait_ge(*bank_left(it, "v", j))
                    product(bank_of("v", j), 1 - par, a, CHUNK_AT[4 + j], v_full)

                def turn(bank, src, done):
                    for t in range(4):
                        i = nc.tensor.transpose(bank[:, 128 * t:128 * t + 128], src(t), ident[:])
                    i.then_inc(done, 1)

                def turn_qk(g):
                    pe.wait_ge(qk_ready, nk(a, 4, g) + 1)
                    pe.wait_ge(*bank_left(it, "turn_qk", g))
                    turn(bank_of("turn_qk", g), lambda t: u[:, 1 - par, g, 128 * t:128 * t + 128], qkT_full)

                def scores(s):
                    pe.wait_ge(qkT_ready, nk(a, 4, 2 * s + 2))
                    pe.wait_ge(sc_out, nk(a, 4, 2 * s))
                    for e in range(2):
                        nc.tensor.matmul(by_head(C[e][:], 4), identb[:], maskb[:].unsqueeze(1).broadcast_to([128, 4, 128]),
                                         start=True, stop=False, skip_group_check=True)
                    for t in range(4):
                        for e in range(2):
                            r = slice(64 * e, 64 * e + 64)
                            i = nc.tensor.matmul(C[e][:, 128 * t:128 * t + 128], qkT[r, 2 * s, t], qkT[r, 2 * s + 1, t],
                                                 start=False, stop=(t == 3), skip_group_check=True)
                            if t == 3:
                                i.then_inc(sc_full, 1)

                def turn_p(g):
                    pe.wait_ge(exp_done, nk(c_, 4, g) + 1)
                    pe.wait_ge(*bank_left(it, "turn_p", g))
                    turn(bank_of("turn_p", g), lambda t: P[:, par, g, t], PT_full)

                def values(g):
                    s, e = g // 2, g % 2
                    pe.wait_ge(PT_ready, nk(c_, 4, g) + 1)
                    pe.wait_ge(v_ready, nk(c_, 2, 2))
                    pe.wait_ge(pv_out, nk(c_, 4, g))
                    for t in range(4):
                        i = nc.tensor.matmul(Dk[:, (DH + 1) * t:(DH + 1) * (t + 1)], PT[:, e, t],
                                             v[:, par, 8 * s + 2 * t + e], start=True, stop=True)
                    i.then_inc(pv_full, 1)

                def turn_o(s):
                    pe.wait_ge(pv_out, nk((c_, m)[s], 4, 2 * s + 2))
                    pe.wait_ge(*bank_left(it, "turn_o", s))
                    turn(bank_of("turn_o", s), lambda t: O[:, 512 * s + 128 * t:512 * s + 128 * t + 128], OT_full)

                def up(k):
                    pe.wait_ge(xf_ready, n_(f) + 1)
                    pe.wait_ge(*bank_left(it, "up", k))
                    nc.tensor.matmul(bank_of("up", k)[:, 0:DI], xf[:], weights(f, W1_AT + DI * (1 - k), DI), start=True,
                                     stop=True).then_inc(gv_full, 1)

                if weigh:
                    turn_p(0)
                if score:
                    turn_qk(0)
                if project:
                    pe.wait_ge(W_split, (n // NB) * (NB // 2) + NB // 2 + START)
                    pe.wait_ge(xs_split, n_(n) + 1)
                    chunk(0)
                if finish:
                    turn_o(1)
                if score:
                    turn_qk(1)
                if weigh:
                    values(0)
                if score:
                    scores(0)
                if feed:
                    up(0)
                if project:
                    chunk(1)
                if finish:
                    pe.wait_ge(w_ready, (m // NB) * (16 * LOADS) + 16 * LOADS)
                    pe.wait_ge(OT_ready, nk(m, 2, 2))
                    pe.wait_ge(*bank_left(it, "Wo"))
                    for k in range(INNER // 128):
                        i = nc.tensor.matmul(E[:, 0:D], OT[:, k // 4, k % 4], weights(m, WO_AT + k * D, D),
                                             start=(k == 0), stop=(k == INNER // 128 - 1))
                    i.then_inc(Wo_full, 1)
                if weigh:
                    turn_p(1)
                if score:
                    v_chunk(0)
                if score:
                    turn_qk(2)
                if feed:
                    up(1)
                if finish:
                    pe.wait_ge(*bank_left(it, "xs"))
                    nc.tensor.matmul(E[:, 0:64], ident[:], row_of(H, m)[:, 0:64], start=True, stop=True)
                    nc.tensor.matmul(E[:, 64:128], shf[:], row_of(H, m)[:, 64:128], start=True, stop=True).then_inc(xs_full, 1)
                if score:
                    turn_qk(3)
                if weigh:
                    values(1)
                if score:
                    v_chunk(1)
                if weigh:
                    turn_p(2)
                    turn_p(3)
                if project:
                    chunk(2)
                if finish:
                    pe.wait_ge(*bank_left(it, "xhT"))
                    nc.tensor.transpose(E[:, 0:S], xh[:, par], ident[:]).then_inc(xhT_full, 1)
                if weigh:
                    values(2)
                if feed:
                    pe.wait_ge(hh_ready, n_(f) + 1)
                    pe.wait_ge(*bank_left(it, "turn_h"))
                    for t in range(KT2):
                        w = min(128, DI - 128 * t)
                        i = nc.tensor.transpose(bank_of("turn_h", 0)[0:w, 128 * t:128 * t + 128], hh[:, 128 * t:128 * t + w],
                                                ident[:])
                    i.then_inc(hT_full, 1)
                if ahead:
                    pe.wait_ge(xw_ready, n_(it + 1) + 1)
                    pe.wait_ge(*bank_left(it, "xT"))
                    nc.tensor.transpose(E[:, 0:S], xw[:, 1 - par], ident[:]).then_inc(xT_full, 1)
                if score:
                    scores(1)
                if project:
                    chunk(3)
                if weigh:
                    turn_o(0)
                    values(3)
                if feed:
                    pe.wait_ge(hT_ready, n_(f) + 1)
                    pe.wait_ge(*bank_left(it, "down"))
                    for t in range(KT2):
                        w = min(128, DI - 128 * t)
                        i = nc.tensor.matmul(E[:, 0:D], hT[0:w, t], weights(f, W2_AT + t * D, D, w), start=(t == 0),
                                             stop=(t == KT2 - 1))
                    i.then_inc(y_full, 1)

            pipeline(pe, step)


def rotary_constants():
    f = np.float32
    half = np.arange(0, DH, 2, dtype=f)
    inv_freq = (f(1.0) / f(10000.0) ** (half / f(DH))).astype(f)
    t = np.arange(S, dtype=f)
    freqs = t[:, None] * inv_freq[None, :]
    base = ((half + f(0.4 * DH)) / f(1.4 * DH)).astype(f)
    power = ((t - S // 2) / f(WINDOW // 2)).astype(f)
    scale = (base[None, :] ** power[:, None]).astype(f)
    cos, sin = np.cos(freqs), np.sin(freqs)
    q = np.stack([np.concatenate([cos * scale * f(8)] * 2, -1), np.concatenate([cos / scale] * 2, -1)], 1)
    s = np.stack([np.concatenate([-sin * scale * f(8), sin * scale * f(8)], -1),
                  np.concatenate([-sin / scale, sin / scale], -1)], 1)
    return q.astype(f), s.astype(f)


def band_mask():
    i, j = np.arange(S)[:, None], np.arange(S)[None, :]
    return np.where((i < j) | (i > j + WINDOW), NEG, 0.0).astype(np.float32)


_INS = ['x', 'ctx_1024', 'g_xattn', 'g_ffn', 'L0_xattn_Wq', 'L0_xattn_bq', 'L0_xattn_qk_b', 'L0_xattn_Wv',
        'L0_xattn_bv', 'L0_ffn_Wqkv', 'L0_ffn_q_scale', 'L0_ffn_k_scale', 'L0_ffn_Wo', 'L0_ffn_ln_g', 'L0_ffn_ln_b',
        'L0_ffn_W1', 'L0_ffn_b1', 'L0_ffn_W2', 'L0_ffn_b2']

_TRANSPOSED = ('ctx_1024', 'L0_xattn_Wq', 'L0_xattn_Wv', 'L0_ffn_ln_g', 'L0_ffn_ln_b')


def kernel(**inputs):
    import concourse.bacc as _bacc
    from concourse.bass_utils import run_bass_kernel_spmd as _run

    nc = _bacc.Bacc("TRN2", target_bir_lowering=False, num_devices=1)
    arrays, args = {}, []
    cos, sin = rotary_constants()
    consts = {"rot_cos": cos, "rot_sin": sin, "band": band_mask(), "eye": np.eye(128, dtype=np.float32),
              "shift": np.eye(128, k=1, dtype=np.float32)}
    for name in _INS + list(consts):
        a = np.asarray(consts[name] if name in consts else inputs[name])
        if name in _TRANSPOSED:
            a = a.swapaxes(-1, -2)
        a = np.ascontiguousarray(a)
        arrays[f"in_{name}_dram"] = a
        args.append(nc.dram_tensor(f"in_{name}_dram", a.shape, mybir.dt.from_np(a.dtype), kind="ExternalInput").ap())
    out = nc.dram_tensor("out_dram", (NB, S, D), mybir.dt.float32, kind="ExternalOutput").ap()
    program(nc, *args, out)
    return _run(nc, [arrays], core_ids=[0]).results[0]["out_dram"]
```

```python
import numpy as np
import concourse.bass as bass
from concourse import mybir
from contextlib import ExitStack

L, NB, S, D = 6, 16, 128, 128
N = L * NB
HEADS, DH, WINDOW = 16, 64, 32
INNER = HEADS * DH
DI = int(D * 4 * 2 / 3)
DI_EVEN = DI + DI % 2
HC = 512 // DH
NCH = 2 * INNER // 512
CHUNK_AT = [0, INNER, 512, INNER + 512, 2 * INNER, 2 * INNER + 512]
QKV = 3 * INNER
W1_AT = QKV
BLOCK = -(-(QKV + 2 * DI) // (NB // 2))
W_SPLIT_SIZE = BLOCK * (NB // 2)
WO_AT = 0
W2_AT = WO_AT + (INNER // 128) * D
KT2 = -(-DI // 128)
B1_AT = W2_AT + KT2 * D
B2_AT = B1_AT + 2 * DI
W_SIZE = B2_AT + D
LOADS = 5
FINISH_AT = [N, N + 1, N + 2, N + 3]
START = 16
GB = 4
CROSS_HEADS = 16
NEG = -1e30
SS_SCALE_LOG2 = 20


def program(nc, x, ctxT, Wqkv, Wo, W1, b1, W2, b2, by_feature, every_token, shape_consts, out):
    F32, F32R, BF16 = mybir.dt.float32, mybir.dt.float32r, mybir.dt.bfloat16
    ALU, ACT, AX = mybir.AluOpType, mybir.ActivationFunctionType, mybir.AxisListType.X
    ds = bass.ds
    es = ExitStack()

    def sb(name, shape, dt=F32):
        return es.enter_context(nc.sbuf_tensor(name, shape, dt))

    def sem(name):
        return es.enter_context(nc.semaphore(name))

    with es:
        H = sb("H", [128, NB, D])
        X1 = sb("X1", [128, NB, D])
        Wraw = sb("Wraw", [128, W_SPLIT_SIZE])
        Wh = sb("Wh", [128, 2 * W_SPLIT_SIZE], F32R)
        Wl = sb("Wl", [128, 2 * W_SPLIT_SIZE], F32R)
        WB = sb("WB", [128, 2 * W_SIZE])
        TC = sb("TC", [128, L, 2, DH])
        TS = sb("TS", [128, L, 2, DH])
        sc = sb("shape_constants", [128, 5 * 128])
        rc, rsn = (sc[:, 128 * i:128 * i + 128].rearrange("p (w d) -> p w d", w=2) for i in (0, 1))
        maskf, ident, shf = (sc[:, 128 * i:128 * i + 128] for i in (2, 3, 4))
        fc = sb("feature_columns", [128, 2 * 128 + 3 + 2 * L])
        wqT, wvT, bqc = fc[:, 0:128], fc[:, 128:256], fc[:, 256:259]
        lng, lnb = fc[:, 259:259 + L], fc[:, 259 + L:259 + 2 * L]
        ev = sb("every_token_rows", [128, 128 + 2 + 2 * L * DH])
        bvb, gate2 = ev[:, 0:128], ev[:, 128:130]
        qs = ev[:, 130:130 + 2 * L * DH].rearrange("p (w l d) -> p w l d", w=2, l=L)
        identb = sb("identb", [128, 128], BF16)
        maskb = sb("maskb", [128, 128], BF16)
        tg = sb("tg", [128, 2])
        bqs = sb("bqs", [128, 1])
        xw = sb("xw", [128, 2, D])
        xsh = sb("xsh", [128, 2, S], F32R)
        xsl = sb("xsl", [128, 2, S], F32R)
        sq = sb("sq", [128, 2, 512])
        ss = sb("ss", [128, 2, 4 * HC])
        ssc = sb("ssc", [128, 2, 4 * HC])
        lnv = sb("lnv", [128, 2, 4 * HC])
        rn = sb("rn", [128, 2, 4 * HC])
        u = sb("u", [128, 2, NCH, 512])
        t2 = sb("t2", [128, 2, 512])
        qkT = sb("qkT", [128, NCH, 4, 128])
        nm = sb("nm", [128, 16])
        rs = sb("rs", [128, 16])
        P = sb("P", [128, 2, 4, 4, 128])
        PT = sb("PT", [128, 2, 4, 128])
        v = sb("v", [128, 2, HEADS, DH + 1])
        O = sb("O", [128, INNER])
        raw = sb("raw", [128, 2, 512])
        OT = sb("OT", [128, 2, 4, 128])
        bst = sb("bst", [128, 2, 2, 6])
        mv = sb("mv", [128, 2, 2])
        lv = sb("lv", [128, 2])
        rstd = sb("rstd", [128, 2])
        xh = sb("xh", [128, 2, D])
        xf = sb("xf", [128, S])
        xfh = sb("xfh", [128, S], F32R)
        xfl = sb("xfl", [128, S], F32R)
        gate = sb("gate", [128, DI])
        value = sb("value", [128, DI])
        hh = sb("hh", [128, DI])
        hT = sb("hT", [128, KT2, 128])
        yb = sb("yb", [128, D])
        ctxS = P[:, 0].rearrange("p g h k -> p (g h) k")
        cT = [t2[:, g] for g in range(2)]
        slots = [[u[:, g, j] for j in range(NCH)] + [qkT[:, j].rearrange("p t n -> p (t n)")
                                                        for j in (2 * g, 2 * g + 1)] + [(sq, raw)[g][:, 0]]
                 for g in range(2)]
        xh4, xhT4, qT4, vT4, p4, pT4, v4 = ([slots[g][j] for g in range(2)] for j in range(7))
        st4 = sb("st4", [128, 2, GB, 6])
        mv4 = sb("mv4", [128, 2, GB, 2])
        lv4 = sb("lv4", [128, 2, GB])
        rstd4 = sb("rstd4", [128, 2, GB])
        mx4 = sb("mx4", [128, 2, GB])
        nm4 = sb("nm4", [128, 2, GB])
        sum4 = sb("sum4", [128, 2, GB])
        rc4 = sb("rc4", [128, 2, GB])
        rg4 = sb("rg4", [128, 2, GB])
        cols = sb("cols", [128, 2])
        eps_col, exp_col = cols[:, 0:1], cols[:, 1:2]

        def bank(name):
            return es.enter_context(nc.psum_tensor("bank_" + name, [128, 512], F32))

        A = [bank("A0"), bank("A1")]
        B = [bank("B0"), bank("B1")]
        C = [bank("C0"), bank("C1")]
        Dk = bank("D")
        E = bank("E")
        X_, V_, VT_, Q_ = [A[0], A[1]], [B[0], B[1]], [C[0], C[1]], [Dk, E]

        in_ready, rest_ready, raw_loaded, w_ready, out_done = (
            sem(s) for s in ("in_ready", "rest_ready", "raw_loaded", "w_ready", "out_done"))
        ch_full = sem("ch_full")
        v_full = sem("v_full")
        qkT_full = sem("qkT_full")
        sc_full = sem("sc_full")
        PT_full = sem("PT_full")
        pv_full = sem("pv_full")
        OT_full = sem("OT_full")
        Wo_full = sem("Wo_full")
        xT_full = sem("xT_full")
        xs_full = sem("xs_full")
        xhT_full = sem("xhT_full")
        gv_full = sem("gv_full")
        hT_full = sem("hT_full")
        y_full = sem("y_full")
        PE_SEMS = [ch_full, v_full, qkT_full, sc_full, PT_full, pv_full, OT_full, Wo_full, xT_full, xs_full, xhT_full,
                   gv_full, hT_full, y_full]
        rot_done = sem("rot_done")
        ss_done = sem("ss_done")
        ss_ready = sem("ss_ready")
        mx_done = sem("mx_done")
        sc_out = sem("sc_out")
        rs_done = sem("rs_done")
        pv_out = sem("pv_out")
        res_done = sem("res_done")
        bst_done = sem("bst_done")
        mv_ready = sem("mv_ready")
        xh_ready = sem("xh_ready")
        xf_done = sem("xf_done")
        xfh_done = sem("xfh_done")
        xf_ready = sem("xf_ready")
        gv_out = sem("gv_out")
        hh_ready = sem("hh_ready")
        y_out = sem("y_out")
        xs_split = sem("xs_split")
        h_ready = sem("h_ready")
        DVE_SEMS = [rot_done, ss_done, ss_ready, mx_done, sc_out, rs_done, pv_out, res_done, bst_done, mv_ready,
                    xh_ready, xf_done, xfh_done, xf_ready, gv_out, hh_ready, y_out, xs_split, h_ready]
        xsh_ready = sem("xsh_ready")
        sq_done = sem("sq_done")
        raw_ready = sem("raw_ready")
        v_ready = sem("v_ready")
        qkT_ready = sem("qkT_ready")
        exp_done = sem("exp_done")
        PT_ready = sem("PT_ready")
        OT_ready = sem("OT_ready")
        ln_done = sem("ln_done")
        rn_ready = sem("rn_ready")
        lv_done = sem("lv_done")
        rstd_ready = sem("rstd_ready")
        gelu_done = sem("gelu_done")
        hT_ready = sem("hT_ready")
        high_ready = sem("high_ready")
        ACT_SEMS = [xsh_ready, sq_done, raw_ready, v_ready, qkT_ready, exp_done, PT_ready, OT_ready, ln_done, rn_ready,
                    lv_done, rstd_ready, gelu_done, hT_ready, high_ready]
        xw_ready = sem("xw_ready")
        t2_done = sem("t2_done")
        add_done = sem("add_done")
        qk_ready = sem("qk_ready")
        W_split = sem("W_split")
        POOL_SEMS = [xw_ready, t2_done, add_done, qk_ready, W_split]
        tables_ready, tanh_done, consts_done = sem("tables_ready"), sem("tanh_done"), sem("consts_done")
        bqs_ready, consts_act = sem("bqs_ready"), sem("consts_act")
        c_st, c_mv, c_lv, c_rstd, c_xh, c_ctx = (sem(s) for s in ("c_st", "c_mv", "c_lv", "c_rstd", "c_xh", "c_ctx"))
        c_xT, c_xTs, c_qv, c_v, c_qvs, c_vs = (sem(s) for s in ("c_xT", "c_xTs", "c_qv", "c_v", "c_qvs", "c_vs"))
        c_sc, c_mx, c_nm, c_exp, c_rc, c_rg, c_pT, c_pTs, c_o, c_x1 = (
            sem(s) for s in ("c_sc", "c_mx", "c_nm", "c_exp", "c_rc", "c_rg", "c_pT", "c_pTs", "c_o", "c_x1"))
        fin_ready = sem("fin_ready")
        wait_met = sem("wait_met")

        def n_(n):
            return n + START

        def nk(n, per, k):
            return n * per + k + START

        def pipeline(eng, step):
            last = N - NB + 1

            def peeled(it):
                step(it, it % 2, *[0 <= it - lag < N for lag in (0, 1, 2, 3, 4, -1)], it % 2 == 1 and 1 <= it < last)

            for it in range(-1, 5):
                peeled(it)
            with eng.Fori(0, (last - 5) // 2) as pair:
                step(pair * 2 + 5, 1, True, True, True, True, True, True, True)
                step(pair * 2 + 6, 0, True, True, True, True, True, True, False)
            with eng.Fori(0, (N - 1 - last) // 2) as pair:
                step(pair * 2 + last, 1, True, True, True, True, True, True, False)
                step(pair * 2 + last + 1, 0, True, True, True, True, True, True, False)
            for it in range(N - 1, N + 4):
                peeled(it)

        USERS = {"chunk": (0, 4, rot_done), "up": (4, 2, gv_out), "v": (1, 2, v_ready),
                 "turn_qk": (1, 4, qkT_ready), "turn_p": (2, 4, PT_ready), "turn_h": (4, 1, hT_ready),
                 "turn_o": (3, 2, OT_ready), ("turn_o", 0): (2, 2, OT_ready),
                 "Wo": (3, 1, res_done), "xs": (3, 1, xh_ready), "xhT": (3, 1, xf_done), "xT": (-1, 1, xs_split),
                 "down": (4, 1, y_out)}
        BANK_USERS = [
            (A[0], [("chunk", 0), ("up", 0), ("v", 0), ("chunk", 2)]),
            (A[1], [("chunk", 1), ("up", 1), ("v", 1), ("chunk", 3)]),
            (B[0], [("turn_qk", 0), ("turn_qk", 1), ("turn_qk", 2), ("turn_p", 2), ("turn_h", 0), ("turn_o", 0)]),
            (B[1], [("turn_p", 0), ("turn_o", 1), ("turn_p", 1), ("turn_qk", 3), ("turn_p", 3)]),
            (E, [("Wo", 0), ("xs", 0), ("xhT", 0), ("xT", 0), ("down", 0)])]

        def bank_of(kind, k):
            return next(b for b, users in BANK_USERS if (kind, k) in users)

        def bank_left(it, kind, k=0):
            users = next(users for _, users in BANK_USERS if (kind, k) in users)
            place = users.index((kind, k))
            for back in range(1, 4 * len(users)):
                turns, at = divmod(place - back, len(users))
                other, ok = users[at]
                lag, per, counter = USERS.get(users[at], USERS[other])
                n = it + turns - lag
                if not isinstance(it, int) or 0 <= n < N:
                    return counter, nk(n, per, ok) + 1
            return USERS[kind][2], START

        def weights(n, at, size, rows=128):
            return WB[0:rows, ds(((n // NB) % 2) * W_SIZE + at, size)]

        def layer(n):
            return ds(n // NB, 1)

        def row_of(t, n):
            return t[:, ds(n % NB, 1)].rearrange("p o d -> p (o d)")

        def halves(ap):
            return ap.rearrange("p (h a d) -> p h a d", h=HC, a=2)

        def by_head(ap, n=HC):
            return ap.rearrange("p (h d) -> p h d", h=n)

        def spread(ap, n, m):
            return ap.unsqueeze(2).broadcast_to([128, n, m])

        N_INPUTS = 5

        def raw_block(block):
            return Wraw[:, ds(block * BLOCK, BLOCK)]

        def part_block(W, k, block):
            return W[:, ds((k // (NB // 2)) % 2 * W_SPLIT_SIZE + block * BLOCK, BLOCK)]

        PAIR = 2 * GB

        def tiles(t):
            return [t[:, 128 * j:128 * j + 128] for j in range(GB)]

        block = es.enter_context(nc.Block())

        @block.sync
        def _(sp):
            sp.dma_start(H[:, 0:PAIR], x[0:PAIR].rearrange("b s d -> s b d")).then_inc(in_ready, 16)
            sp.dma_start(ctxS[:, 0:PAIR], ctxT[0:PAIR].rearrange("b d s -> d b s")).then_inc(in_ready, 16)
            sp.dma_start(sc[:], shape_consts).then_inc(in_ready, 16)
            sp.dma_start(fc[:], by_feature).then_inc(in_ready, 16)
            sp.dma_start(ev[:], every_token.partition_broadcast(128)).then_inc(in_ready, 16)
            sp.sem_inc(rest_ready, START)
            sp.dma_start(H[:, PAIR:NB], x[PAIR:NB].rearrange("b s d -> s b d")).then_inc(rest_ready, 16)
            sp.dma_start(ctxS[:, PAIR:NB], ctxT[PAIR:NB].rearrange("b d s -> d b s")).then_inc(rest_ready, 16)
            for l in range(L):
                if l >= 1:
                    sp.wait_ge(W_split, NB // 2 * l + START)
                sp.dma_start(Wraw[:, 0:QKV], Wqkv[l]).then_inc(raw_loaded, 16)
                sp.dma_start(Wraw[:, W1_AT:W1_AT + 2 * DI], W1[l]).then_inc(raw_loaded, 16)
                if l >= 1:
                    sp.wait_ge(w_ready, 16 * LOADS * l)
                if l >= 2:
                    sp.wait_ge(h_ready, NB * l + START)
                o = (l % 2) * W_SIZE
                sp.dma_start(WB[:, o + WO_AT:o + W2_AT].rearrange("p (k n) -> p k n", n=D),
                             Wo[l].rearrange("(k p) n -> p k n", p=128)).then_inc(w_ready, 16)
                sp.dma_start(WB[:, o + W2_AT:o + W2_AT + (KT2 - 1) * D].rearrange("p (k n) -> p k n", n=D),
                             W2[l, 0:(KT2 - 1) * 128].rearrange("(k p) n -> p k n", p=128)).then_inc(w_ready, 16)
                sp.dma_start(WB[0:DI - (KT2 - 1) * 128, o + W2_AT + (KT2 - 1) * D:o + B1_AT],
                             W2[l, (KT2 - 1) * 128:DI]).then_inc(w_ready, 16)
                sp.dma_start(WB[:, o + B1_AT:o + B2_AT], b1[l].partition_broadcast(128)).then_inc(w_ready, 16)
                sp.dma_start(WB[:, o + B2_AT:o + W_SIZE], b2[l].partition_broadcast(128)).then_inc(w_ready, 16)
            for q in range(4):
                sp.wait_ge(fin_ready, q + 1)
                sp.dma_start(out[4 * q:4 * q + 4].rearrange("b s d -> s b d"),
                             X1[:, 4 * q:4 * q + 4]).then_inc(out_done, 16)
            sp.wait_ge(out_done, 64)

        @block.gpsimd
        def _(pool):
            for s in POOL_SEMS:
                pool.sem_inc(s, START)

            def step(it, par, project, score, weigh, finish, feed, ahead, split):
                n = it

                def rotate(c):
                    w = c % 2
                    pool.wait_ge(raw_ready, nk(n, 4, c) + 1)
                    pool.sem_inc(wait_met, 1)
                    nc.gpsimd.tensor_tensor(halves(t2[:, w]), halves(raw[:, w])[:, :, ::-1, :],
                                            TS[:, layer(n), w].broadcast_to([128, HC, DH]).rearrange(
                                                "p h (a d) -> p h a d", a=2), ALU.mult).then_inc(t2_done, 1)
                    pool.wait_ge(t2_done, nk(n, 4, c) + 1)
                    pool.wait_ge(rot_done, nk(n, 4, c) + 1)
                    nc.gpsimd.tensor_tensor(u[:, par, c], u[:, par, c], t2[:, w], ALU.add).then_inc(add_done, 1)

                def normalise(half):
                    pool.wait_ge(rn_ready, nk(n, 2, half) + 1)
                    for c in (2 * half, 2 * half + 1):
                        pool.wait_ge(add_done, nk(n, 4, c) + 1)
                        nc.gpsimd.tensor_tensor(by_head(u[:, par, c]), by_head(u[:, par, c]),
                                                spread(rn[:, par, HC * c:HC * c + HC], HC, DH),
                                                ALU.mult).then_inc(qk_ready, 1)

                if ahead:
                    pool.wait_ge(h_ready, n_(it + 1) + 1)
                    pool.wait_ge(xT_full, n_(it + 1) - 1)
                    pool.sem_inc(wait_met, 1)
                    nc.gpsimd.tensor_copy(xw[:, 1 - par], row_of(H, it + 1)).then_inc(xw_ready, 1)
                if project:
                    rotate(0)
                    rotate(1)
                    normalise(0)
                if split:
                    lower_part((it - 1) // 2 + NB // 2, (it % NB) // 2)
                if project:
                    rotate(2)
                    rotate(3)
                    normalise(1)

            def lower_part(k, block):
                pool.wait_ge(high_ready, k + 1 + START)
                pool.sem_inc(wait_met, 1)
                nc.gpsimd.tensor_tensor(part_block(Wl, k, block), raw_block(block), part_block(Wh, k, block),
                                        ALU.subtract).then_inc(W_split, 1)

            pool.wait_ge(in_ready, 16 * N_INPUTS)
            pool.sem_inc(c_ctx, START)
            with pool.Fori(0, NB // PAIR) as pair:
                pool.wait_ge(rest_ready, pair * 32 + START)
                for j in range(2):
                    g = pair * 2 + j
                    pool.wait_ge(c_v, g - 1 + START)
                    pool.sem_inc(wait_met, 1)
                    nc.gpsimd.tensor_copy(cT[j], ctxS[:, ds(g * GB, GB)].rearrange("p b d -> p (b d)")).then_inc(c_ctx, 1)
                for i in range(4):
                    lower_part(pair * 4 + i, pair * 4 + i)
            for w in range(2):
                nc.gpsimd.tensor_tensor(TC[:, :, w], qs[:, w], rc[:, w].unsqueeze(1).broadcast_to([128, L, DH]), ALU.mult)
                for a in range(2):
                    o, i = 32 * a, 32 * (1 - a)
                    nc.gpsimd.tensor_tensor(TS[:, :, w, o:o + 32], qs[:, w, :, i:i + 32],
                                            rsn[:, w, o:o + 32].unsqueeze(1).broadcast_to([128, L, 32]),
                                            ALU.mult).then_inc(tables_ready, 1)
            pool.wait_ge(tables_ready, 4)
            pipeline(pool, step)

        @block.scalar
        def _(act):
            for s in ACT_SEMS + [c_lv, c_rstd, c_xTs, c_qvs, c_exp, c_pTs]:
                act.sem_inc(s, START)
            act.wait_ge(in_ready, 16 * N_INPUTS)
            nc.scalar.activation(tg[:], gate2[:], ACT.Tanh).then_inc(tanh_done, 1)
            nc.scalar.copy(identb[:], ident[:]).then_inc(consts_act, 1)
            nc.scalar.copy(maskb[:], maskf[:]).then_inc(consts_act, 1)
            nc.scalar.preload_act_table_set("natural_log_exp_and_others")

            def upper_part(k, block):
                act.sem_inc(wait_met, 1)
                nc.scalar.copy(part_block(Wh, k, block), raw_block(block)).then_inc(high_ready, 1)

            def cross_rstd(pair, s):
                for j in range(2):
                    k = pair * 4 + 2 * s + j + START
                    act.wait_ge(c_mv, k + 1)
                    nc.scalar.activation(lv4[:, j], mv4[:, j, :, 1], ACT.Ln, bias=eps_col).then_inc(c_lv, 1)
                    act.wait_ge(c_lv, k + 1)
                    nc.scalar.activation(rstd4[:, j], lv4[:, j], ACT.Exp, scale=-0.5).then_inc(c_rstd, 1)

            act.wait_ge(consts_done, 1)
            act.wait_ge(bqs_ready, 1)
            with act.Fori(0, NB // PAIR) as pair:
                cross_rstd(pair, 0)
                act.wait_ge(raw_loaded, 32)
                upper_part(pair * 4, pair * 4)
                upper_part(pair * 4 + 1, pair * 4 + 1)
                for j in range(2):
                    act.wait_ge(c_xT, pair * 2 + j + 1 + START)
                    nc.scalar.copy(xhT4[j], X_[j][:]).then_inc(c_xTs, 1)
                upper_part(pair * 4 + 2, pair * 4 + 2)
                upper_part(pair * 4 + 3, pair * 4 + 3)
                for j in range(2):
                    act.wait_ge(c_qv, pair * 2 + j + 1 + START)
                    nc.scalar.activation(qT4[j], Q_[j][:], ACT.Identity, bias=bqs[:])
                    nc.scalar.activation(vT4[j], VT_[j][:], ACT.Identity, bias=bqc[:, 2:3]).then_inc(c_qvs, 1)
                for j in range(2):
                    act.wait_ge(c_nm, pair * 2 + j + 1 + START)
                    for t, (dst, src) in enumerate(zip(tiles(p4[j]), tiles(X_[j]))):
                        i = nc.scalar.activation(dst, src, ACT.Exp, bias=nm4[:, j, t:t + 1],
                                                 scale=(D / CROSS_HEADS) ** -0.5, accum_out=sum4[:, j, t:t + 1])
                    i.then_inc(c_exp, 1)
                for j in range(2):
                    act.wait_ge(c_pT, pair * 2 + j + 1 + START)
                    nc.scalar.copy(pT4[j], V_[j][:]).then_inc(c_pTs, 1)
                cross_rstd(pair, 1)

            def step(it, par, project, score, weigh, finish, feed, ahead, split):
                n, a, c_, m, f = (it - k for k in range(5))

                def square_and_copy(c):
                    act.wait_ge(ch_full, nk(n, 4, c) + 1)
                    act.wait_ge(ss_done, nk(n, 4, c) - 1)
                    nc.scalar.activation(sq[:, c % 2], A[c % 2][:], ACT.Square).then_inc(sq_done, 1)
                    act.wait_ge(t2_done, nk(n, 4, c) - 1)
                    nc.scalar.copy(raw[:, c % 2], A[c % 2][:]).then_inc(raw_ready, 1)

                def norms(half):
                    b, p = (n, par) if half == 0 else (a, 1 - par)
                    w = slice(2 * HC * half, 2 * HC * half + 2 * HC)
                    act.wait_ge(ss_ready, nk(b, 2, half) + 1)
                    nc.scalar.activation(lnv[:, p, w], ssc[:, p, w], ACT.Ln,
                                         scale=float(2 ** SS_SCALE_LOG2)).then_inc(ln_done, 1)
                    act.wait_ge(ln_done, nk(b, 2, half) + 1)
                    act.wait_ge(qk_ready, nk(b, 4, 2 * half - 6))
                    nc.scalar.activation(rn[:, p, w], lnv[:, p, w], ACT.Exp, scale=-0.5,
                                         bias=exp_col).then_inc(rn_ready, 1)

                def v_out(j):
                    act.wait_ge(v_full, nk(a, 2, j) + 1)
                    act.wait_ge(pv_full, nk(a, 4, -4))
                    nc.scalar.copy(v[:, 1 - par, HC * j:HC * j + HC, 0:DH], by_head(A[j][:])).then_inc(v_ready, 1)

                def qk_out(g):
                    act.wait_ge(qkT_full, nk(a, 4, g) + 1)
                    act.wait_ge(sc_full, nk(a, 4, -2 if g < 2 else 0))
                    nc.scalar.copy(qkT[:, g].rearrange("p t n -> p (t n)"), bank_of("turn_qk", g)[:]).then_inc(qkT_ready, 1)

                def exp(g):
                    b, p = (a, 1 - par) if g < 2 else (c_, par)
                    act.wait_ge(sc_out, nk(b, 4, g) + 1)
                    pg = P[:, p, g].rearrange("p h k -> p (h k)")
                    nc.scalar.activation(pg, pg, ACT.Exp).then_inc(exp_done, 1)

                def p_out(g):
                    act.wait_ge(PT_full, nk(c_, 4, g) + 1)
                    act.wait_ge(pv_full, nk(c_, 4, g) - 1)
                    nc.scalar.copy(PT[:, g % 2].rearrange("p h k -> p (h k)"),
                                   bank_of("turn_p", g)[:]).then_inc(PT_ready, 1)

                def o_out(s):
                    b = (c_, m)[s]
                    act.wait_ge(OT_full, nk(b, 2, s) + 1)
                    act.wait_ge(Wo_full, n_(b))
                    nc.scalar.copy(OT[:, s].rearrange("p t n -> p (t n)"), bank_of("turn_o", s)[:]).then_inc(OT_ready, 1)

                def gelu():
                    act.wait_ge(gv_out, nk(f, 2, 0) + 1)
                    nc.scalar.activation(gate[:], gate[:], ACT.Gelu).then_inc(gelu_done, 1)

                def h_out():
                    act.wait_ge(hT_full, n_(f) + 1)
                    act.wait_ge(y_full, n_(f))
                    nc.scalar.copy(hT[:, 0:KT2 - 1].rearrange("p t n -> p (t n)"),
                                   bank_of("turn_h", 0)[:, 0:(KT2 - 1) * 128])
                    nc.scalar.copy(hT[0:DI - (KT2 - 1) * 128, KT2 - 1],
                                   bank_of("turn_h", 0)[0:DI - (KT2 - 1) * 128,
                                                        (KT2 - 1) * 128:KT2 * 128]).then_inc(hT_ready, 1)

                if weigh:
                    p_out(0)
                if score:
                    qk_out(0)
                if finish:
                    o_out(1)
                if score:
                    qk_out(1)
                if project:
                    square_and_copy(0)
                if score:
                    norms(1)
                if weigh:
                    exp(2)
                    exp(3)
                if feed:
                    nc.scalar.preload_act_table(ACT.Gelu)
                    gelu()
                if project:
                    square_and_copy(1)
                if feed:
                    nc.scalar.preload_act_table_set("natural_log_exp_and_others")
                if weigh:
                    p_out(1)
                if project:
                    norms(0)
                if score:
                    v_out(0)
                    qk_out(2)
                if score:
                    qk_out(3)
                if finish:
                    act.wait_ge(mv_ready, n_(m) + 1)
                    nc.scalar.activation(lv[:, par:par + 1], mv[:, par, 1:2], ACT.Ln, bias=eps_col).then_inc(lv_done, 1)
                    act.wait_ge(lv_done, n_(m) + 1)
                    act.wait_ge(xh_ready, n_(m) - 1)
                    nc.scalar.activation(rstd[:, par:par + 1], lv[:, par:par + 1], ACT.Exp,
                                         scale=-0.5).then_inc(rstd_ready, 1)
                if weigh:
                    p_out(2)
                if score:
                    v_out(1)
                if weigh:
                    p_out(3)
                if score:
                    exp(0)
                    exp(1)
                if project:
                    square_and_copy(2)
                if feed:
                    h_out()
                if ahead:
                    act.wait_ge(xT_full, n_(it + 1) + 1)
                    act.wait_ge(ch_full, nk(it + 1, 4, -4))
                    act.wait_ge(v_full, nk(it + 1, 2, -2))
                    nc.scalar.copy(xsh[0:64, 1 - par], E[0:64, 0:S])
                    nc.scalar.copy(xsh[64:128, 1 - par, 1:S], E[64:128, 0:S - 1]).then_inc(xsh_ready, 1)
                if split:
                    act.wait_ge(raw_loaded, (it // NB) * 32 + 64)
                    act.wait_ge(v_full, nk(it - 1, 2, 0))
                    act.wait_ge(gv_full, nk(it - 5, 2, 0))
                    upper_part((it - 1) // 2 + NB // 2, (it % NB) // 2)
                if project:
                    square_and_copy(3)
                if weigh:
                    o_out(0)

            pipeline(act, step)

        @block.vector
        def _(dve):
            for s in DVE_SEMS + [c_st, c_mv, c_xh, c_vs, c_mx, c_nm, c_rc, c_rg, c_x1]:
                dve.sem_inc(s, START)
            nc.vector.memset(eps_col, 1e-5)
            nc.vector.memset(exp_col, 0.5 * SS_SCALE_LOG2 * float(np.log(2.0)))
            nc.vector.memset(v[:, :, :, DH:DH + 1], 1.0)
            nc.vector.memset(Wraw[:, W1_AT + 2 * DI:], 0.0)
            nc.vector.memset(xsh[64:128, :, 0:1].bitcast(F32), 0.0)
            nc.vector.memset(xsl[64:128, :, 0:1].bitcast(F32), 0.0).then_inc(consts_done, 1)
            dve.wait_ge(in_ready, 16 * N_INPUTS)
            nc.vector.tensor_tensor(bqs[:], bqc[:, 0:1], bqc[:, 1:2], ALU.add).then_inc(bqs_ready, 1)

            def cross_norm(pair, s, src, dst, done):
                first = pair * 4 + 2 * s + START
                for j in range(2):
                    for t in range(GB):
                        i = nc.vector.bn_stats(st4[:, j, t], src(j)[t])
                    i.then_inc(c_st, 1)
                for j in range(2):
                    dve.wait_ge(c_st, first + j + 1)
                    dve.sem_inc(wait_met, 1)
                    for t in range(GB):
                        i = nc.vector.bn_aggr(mv4[:, j, t], st4[:, j, t])
                    i.then_inc(c_mv, 1)
                for j in range(2):
                    dve.wait_ge(c_rstd, first + j + 1)
                    dve.wait_ge(c_mv, first + j + 1)
                    for t in range(GB):
                        i = nc.vector.tensor_scalar(dst(j)[t], src(j)[t], mv4[:, j, t, 0:1], rstd4[:, j, t:t + 1],
                                                    ALU.subtract, ALU.mult)
                    i.then_inc(done[0], done[1])

            with dve.Fori(0, NB // PAIR) as pair:
                def rows(t, j):
                    return [t[:, ds(pair * PAIR + GB * j + k, 1)].rearrange("p o d -> p (o d)") for k in range(GB)]

                def by_batch(ap):
                    return ap.rearrange("p (b d) -> p b d", b=GB)

                dve.wait_ge(rest_ready, pair * 32 + START)
                dve.wait_ge(c_xT, pair * 2 + START)
                dve.sem_inc(wait_met, 1)
                cross_norm(pair, 0, lambda j: rows(H, j), lambda j: tiles(xh4[j]), (c_xh, 1))
                for j in range(2):
                    dve.wait_ge(c_v, pair * 2 + j + 1 + START)
                    nc.vector.tensor_tensor(by_batch(v4[j]), by_batch(V_[j][:]),
                                            bvb[:].unsqueeze(1).broadcast_to([128, GB, D]), ALU.add).then_inc(c_vs, 1)
                for j in range(2):
                    dve.wait_ge(c_sc, pair * 2 + j + 1 + START)
                    nc.vector.tensor_reduce(mx4[:, j], by_batch(X_[j][:]), AX, ALU.max).then_inc(c_mx, 1)
                    dve.wait_ge(c_mx, pair * 2 + j + 1 + START)
                    nc.vector.tensor_scalar_mul(nm4[:, j], mx4[:, j], -(D / CROSS_HEADS) ** -0.5).then_inc(c_nm, 1)
                dve.wait_ge(tanh_done, 1)
                for j in range(2):
                    dve.wait_ge(c_exp, pair * 2 + j + 1 + START)
                    nc.vector.reciprocal(rc4[:, j], sum4[:, j]).then_inc(c_rc, 1)
                    dve.wait_ge(c_rc, pair * 2 + j + 1 + START)
                    nc.vector.tensor_scalar_mul(rg4[:, j], rc4[:, j], tg[:, 0:1]).then_inc(c_rg, 1)
                for j in range(2):
                    dve.wait_ge(c_rg, pair * 2 + j + 1 + START)
                    dve.wait_ge(c_o, pair * 2 + j + 1 + START)
                    for t in range(GB):
                        i = nc.vector.scalar_tensor_tensor(out=rows(X1, j)[t], in0=tiles(VT_[j])[t], scalar=rg4[:, j, t:t + 1],
                                                           in1=rows(H, j)[t], op0=ALU.mult, op1=ALU.add)
                    i.then_inc(c_x1, 1)
                dve.wait_ge(c_x1, pair * 2 + 2 + START)
                dve.sem_inc(wait_met, 1)
                cross_norm(pair, 1, lambda j: rows(X1, j), lambda j: rows(H, j), (h_ready, GB))
            dve.wait_ge(tables_ready, 4)

            def step(it, par, project, score, weigh, finish, feed, ahead, split):
                n, a, c_, m, f = (it - k for k in range(5))

                def rotate(c):
                    w = c % 2
                    dve.wait_ge(sq_done, nk(n, 4, c) + 1)
                    nc.vector.tensor_reduce(ss[:, par, HC * c:HC * c + HC], by_head(sq[:, w]), AX,
                                            ALU.add).then_inc(ss_done, 1)
                    dve.wait_ge(raw_ready, nk(n, 4, c) + 1)
                    dve.wait_ge(qkT_full, nk(n, 4, c) - 7)
                    nc.vector.tensor_tensor(by_head(u[:, par, c]), by_head(A[w][:]),
                                            TC[:, layer(n), w].broadcast_to([128, HC, DH]),
                                            ALU.mult).then_inc(rot_done, 1)

                def bound_norms(half):
                    w = slice(2 * HC * half, 2 * HC * half + 2 * HC)
                    dve.wait_ge(ss_done, nk(n, 4, 2 * half + 2))
                    dve.wait_ge(ln_done, nk(n, 2, half) - 3)
                    nc.vector.tensor_scalar_max(ssc[:, par, w], ss[:, par, w], 1e-24).then_inc(ss_ready, 1)

                def maxima(s):
                    for g in (2 * s, 2 * s + 1):
                        dve.wait_ge(sc_full, nk(a, 4, g) + 1)
                        nc.vector.tensor_reduce(nm[:, 4 * g:4 * g + 4], by_head(C[g % 2][:], 4), AX,
                                                ALU.max).then_inc(mx_done, 1)

                def subtract(s):
                    for g in (2 * s, 2 * s + 1):
                        dve.wait_ge(mx_done, nk(a, 4, g) + 1)
                        dve.wait_ge(PT_full, nk(a, 4, g) - 7)
                        nc.vector.tensor_tensor(P[:, 1 - par, g], by_head(C[g % 2][:], 4),
                                                spread(nm[:, 4 * g:4 * g + 4], 4, 128), ALU.subtract).then_inc(sc_out, 1)

                def split_xs():
                    dve.wait_ge(xsh_ready, n_(it + 1) + 1)
                    nc.vector.tensor_tensor(xsl[0:64, 1 - par], E[0:64, 0:S], xsh[0:64, 1 - par], ALU.subtract)
                    nc.vector.tensor_tensor(xsl[64:128, 1 - par, 1:S], E[64:128, 0:S - 1], xsh[64:128, 1 - par, 1:S],
                                            ALU.subtract).then_inc(xs_split, 1)

                def divide(g):
                    s, e = g // 2, g % 2
                    dve.wait_ge(pv_full, nk(c_, 4, g) + 1)
                    heads = by_head(Dk[:, 0:4 * (DH + 1)], 4)
                    nc.vector.reciprocal(rs[:, 4 * g:4 * g + 4], heads[:, :, DH]).then_inc(rs_done, 1)
                    dve.wait_ge(rs_done, nk(c_, 4, g) + 1)
                    dve.wait_ge(OT_full, nk(c_, 2, s) - 1)
                    nc.vector.tensor_tensor(O[:].rearrange("p (s t e d) -> p s t e d", s=2, t=4, e=2)[:, s, :, e, :],
                                            heads[:, :, 0:DH], spread(rs[:, 4 * g:4 * g + 4], 4, DH),
                                            ALU.mult).then_inc(pv_out, 1)

                def bias(k):
                    dve.wait_ge(gv_full, nk(f, 2, k) + 1)
                    dve.wait_ge(hh_ready, n_(f))
                    nc.vector.tensor_tensor((gate, value)[k][:], A[k][:, 0:DI], weights(f, B1_AT + DI * (1 - k), DI),
                                            ALU.add).then_inc(gv_out, 1)

                if project:
                    rotate(0)
                if weigh:
                    divide(0)
                if feed:
                    bias(0)
                if score:
                    maxima(0)
                if project:
                    rotate(1)
                    bound_norms(0)
                if finish:
                    dve.wait_ge(Wo_full, n_(m) + 1)
                    nc.vector.tensor_tensor(row_of(H, m), E[:, 0:D], row_of(H, m), ALU.add).then_inc(res_done, 1)
                if score:
                    subtract(0)
                if feed:
                    bias(1)
                if feed:
                    dve.wait_ge(gelu_done, n_(f) + 1)
                    dve.wait_ge(gv_out, nk(f, 2, 1) + 1)
                    dve.wait_ge(hT_full, n_(f))
                    nc.vector.tensor_tensor(hh[:], value[:], gate[:], ALU.mult).then_inc(hh_ready, 1)
                if finish:
                    dve.wait_ge(res_done, n_(m) + 1)
                    dve.sem_inc(wait_met, 1)
                    nc.vector.bn_stats(bst[:, par, 0], row_of(H, m)[:, 0:64])
                    dve.wait_ge(xs_full, n_(m) + 1)
                    nc.vector.bn_stats(bst[:, par, 1], E[:, 0:64]).then_inc(bst_done, 1)
                    dve.wait_ge(bst_done, n_(m) + 1)
                    dve.wait_ge(lv_done, n_(m) - 1)
                    dve.sem_inc(wait_met, 1)
                    nc.vector.bn_aggr(mv[:, par], bst[:, par]).then_inc(mv_ready, 1)
                if weigh:
                    divide(1)
                if finish:
                    dve.wait_ge(rstd_ready, n_(m) + 1)
                    dve.wait_ge(mv_ready, n_(m) + 1)
                    dve.wait_ge(xhT_full, n_(m) - 1)
                    nc.vector.tensor_scalar(xh[:, par, 0:64], row_of(H, m)[:, 0:64], mv[:, par, 0:1], rstd[:, par:par + 1],
                                            ALU.subtract, ALU.mult)
                    nc.vector.tensor_scalar(xh[:, par, 64:128], E[:, 0:64], mv[:, par, 0:1], rstd[:, par:par + 1],
                                            ALU.subtract, ALU.mult).then_inc(xh_ready, 1)
                if finish:
                    dve.wait_ge(xhT_full, n_(m) + 1)
                    nc.vector.tensor_scalar(xf[:], E[:, 0:S], lng[:, layer(m)], lnb[:, layer(m)], ALU.mult,
                                            ALU.add).then_inc(xf_done, 1)
                    dve.wait_ge(xf_done, n_(m) + 1)
                    dve.wait_ge(gv_full, nk(m, 2, 0))
                    nc.vector.tensor_copy(xfh[:], xf[:]).then_inc(xfh_done, 1)
                    dve.wait_ge(xfh_done, n_(m) + 1)
                    nc.vector.tensor_tensor(xfl[:], xf[:], xfh[:], ALU.subtract).then_inc(xf_ready, 1)
                if project:
                    rotate(2)
                if weigh:
                    divide(2)
                if ahead:
                    split_xs()
                if score:
                    maxima(1)
                    subtract(1)
                if weigh:
                    divide(3)
                if project:
                    rotate(3)
                    bound_norms(1)
                if feed:
                    dve.wait_ge(y_full, n_(f) + 1)
                    nc.vector.tensor_tensor(yb[:], E[:, 0:D], weights(f, B2_AT, D), ALU.add).then_inc(y_out, 1)
                    dve.wait_ge(y_out, n_(f) + 1)
                    nc.vector.tensor_tensor(row_of(H, f), yb[:], row_of(H, f), ALU.add).then_inc(h_ready, 1)
                if not ahead and it in FINISH_AT:
                    finish_quarter(FINISH_AT.index(it))

            def finish_quarter(q):
                dve.wait_ge(h_ready, N + 4 * q + 4 + START)
                x1q = X1[:, 4 * q:4 * q + 4].rearrange("p b d -> p (b d)")
                nc.vector.scalar_tensor_tensor(out=x1q, in0=H[:, 4 * q:4 * q + 4].rearrange("p b d -> p (b d)"),
                                               scalar=tg[:, 1:2], in1=x1q, op0=ALU.mult, op1=ALU.add).then_inc(fin_ready, 1)

            pipeline(dve, step)

        @block.tensor
        def _(pe):
            for s in PE_SEMS + [c_xT, c_qv, c_v, c_sc, c_pT, c_o]:
                pe.sem_inc(s, START)
            pe.wait_ge(in_ready, 16 * N_INPUTS)
            with pe.Fori(0, NB // PAIR) as pair:
                for j in range(2):
                    pe.wait_ge(c_xh, pair * 2 + j + 1 + START)
                    for dst, src in zip(tiles(X_[j]), tiles(xh4[j])):
                        i = nc.tensor.transpose(dst, src, ident[:])
                    i.then_inc(c_xT, 1)
                for j in range(2):
                    pe.wait_ge(c_ctx, pair * 2 + j + 1 + START)
                    nc.tensor.matmul(VT_[j][:], wvT[:], cT[j], start=True, stop=True)
                    for dst, src in zip(tiles(V_[j]), tiles(cT[j])):
                        i = nc.tensor.matmul(dst, src, wvT[:], start=True, stop=True)
                    i.then_inc(c_v, 1)
                    pe.wait_ge(c_xTs, pair * 2 + j + 1 + START)
                    nc.tensor.matmul(Q_[j][:], wqT[:], xhT4[j], start=True, stop=True).then_inc(c_qv, 1)
                for j in range(2):
                    pe.wait_ge(c_qvs, pair * 2 + j + 1 + START)
                    for dst, q, w in zip(tiles(X_[j]), tiles(qT4[j]), tiles(vT4[j])):
                        i = nc.tensor.matmul(dst, q, w, start=True, stop=True)
                    i.then_inc(c_sc, 1)
                for j in range(2):
                    pe.wait_ge(c_exp, pair * 2 + j + 1 + START)
                    pe.wait_ge(c_vs, pair * 2 + j + 1 + START)
                    for dst, src in zip(tiles(V_[j]), tiles(p4[j])):
                        i = nc.tensor.transpose(dst, src, ident[:])
                    i.then_inc(c_pT, 1)
                for j in range(2):
                    pe.wait_ge(c_pTs, pair * 2 + j + 1 + START)
                    for dst, p, w in zip(tiles(VT_[j]), tiles(pT4[j]), tiles(v4[j])):
                        i = nc.tensor.matmul(dst, p, w, start=True, stop=True)
                    i.then_inc(c_o, 1)
            pe.wait_ge(h_ready, NB + START)
            pe.wait_ge(consts_act, 2)

            def step(it, par, project, score, weigh, finish, feed, ahead, split):
                n, a, c_, m, f = (it - k for k in range(5))

                def product(out, xh_, xl_, b, at, size, done):
                    w = ds((b // NB) % 2 * W_SPLIT_SIZE + at, size)
                    nc.tensor.matmul(out, xh_, Wl[:, w], start=True, stop=False)
                    nc.tensor.matmul(out, xl_, Wh[:, w], start=False, stop=False)
                    nc.tensor.matmul(out, xh_, Wh[:, w], start=False, stop=True).then_inc(done, 1)

                def chunk(c):
                    pe.wait_ge(*bank_left(it, "chunk", c))
                    product(bank_of("chunk", c)[:], xsh[:, par], xsl[:, par], n, CHUNK_AT[c], 512, ch_full)

                def v_chunk(j):
                    pe.wait_ge(*bank_left(it, "v", j))
                    product(bank_of("v", j)[:], xsh[:, 1 - par], xsl[:, 1 - par], a, CHUNK_AT[4 + j], 512, v_full)

                def turn(bank, src, done):
                    for t in range(4):
                        i = nc.tensor.transpose(bank[:, 128 * t:128 * t + 128], src(t), ident[:])
                    i.then_inc(done, 1)

                def turn_qk(g):
                    pe.wait_ge(qk_ready, nk(a, 4, g) + 1)
                    pe.wait_ge(*bank_left(it, "turn_qk", g))
                    turn(bank_of("turn_qk", g), lambda t: u[:, 1 - par, g, 128 * t:128 * t + 128], qkT_full)

                def scores(s):
                    pe.wait_ge(qkT_ready, nk(a, 4, 2 * s + 2))
                    pe.wait_ge(sc_out, nk(a, 4, 2 * s))
                    for e in range(2):
                        nc.tensor.matmul(by_head(C[e][:], 4), identb[:], maskb[:].unsqueeze(1).broadcast_to([128, 4, 128]),
                                         start=True, stop=False, skip_group_check=True)
                    for t in range(4):
                        for e in range(2):
                            r = slice(64 * e, 64 * e + 64)
                            i = nc.tensor.matmul(C[e][:, 128 * t:128 * t + 128], qkT[r, 2 * s, t], qkT[r, 2 * s + 1, t],
                                                 start=False, stop=(t == 3), skip_group_check=True)
                            if t == 3:
                                i.then_inc(sc_full, 1)

                def turn_p(g):
                    pe.wait_ge(exp_done, nk(c_, 4, g) + 1)
                    pe.wait_ge(*bank_left(it, "turn_p", g))
                    turn(bank_of("turn_p", g), lambda t: P[:, par, g, t], PT_full)

                def values(g):
                    s, e = g // 2, g % 2
                    pe.wait_ge(PT_ready, nk(c_, 4, g) + 1)
                    pe.wait_ge(v_ready, nk(c_, 2, 2))
                    pe.wait_ge(pv_out, nk(c_, 4, g))
                    for t in range(4):
                        i = nc.tensor.matmul(Dk[:, (DH + 1) * t:(DH + 1) * (t + 1)], PT[:, e, t],
                                             v[:, par, 8 * s + 2 * t + e], start=True, stop=True)
                    i.then_inc(pv_full, 1)

                def turn_o(s):
                    pe.wait_ge(pv_out, nk((c_, m)[s], 4, 2 * s + 2))
                    pe.wait_ge(*bank_left(it, "turn_o", s))
                    turn(bank_of("turn_o", s), lambda t: O[:, 512 * s + 128 * t:512 * s + 128 * t + 128], OT_full)

                def up(k):
                    pe.wait_ge(xf_ready, n_(f) + 1)
                    pe.wait_ge(*bank_left(it, "up", k))
                    product(bank_of("up", k)[:, 0:DI_EVEN], xfh[:], xfl[:], f, W1_AT + DI * (1 - k), DI_EVEN, gv_full)

                if weigh:
                    turn_p(0)
                if score:
                    turn_qk(0)
                if project:
                    pe.wait_ge(W_split, (n // NB) * (NB // 2) + NB // 2 + START)
                    pe.wait_ge(xs_split, n_(n) + 1)
                    chunk(0)
                if finish:
                    turn_o(1)
                if score:
                    turn_qk(1)
                if weigh:
                    values(0)
                if score:
                    scores(0)
                if feed:
                    up(0)
                if project:
                    chunk(1)
                if finish:
                    pe.wait_ge(w_ready, (m // NB) * (16 * LOADS) + 16 * LOADS)
                    pe.wait_ge(OT_ready, nk(m, 2, 2))
                    pe.wait_ge(*bank_left(it, "Wo"))
                    for k in range(INNER // 128):
                        i = nc.tensor.matmul(E[:, 0:D], OT[:, k // 4, k % 4], weights(m, WO_AT + k * D, D),
                                             start=(k == 0), stop=(k == INNER // 128 - 1))
                    i.then_inc(Wo_full, 1)
                if weigh:
                    turn_p(1)
                if score:
                    v_chunk(0)
                if score:
                    turn_qk(2)
                if feed:
                    up(1)
                if finish:
                    pe.wait_ge(*bank_left(it, "xs"))
                    nc.tensor.matmul(E[:, 0:64], shf[:], row_of(H, m)[:, 64:128], start=True, stop=True).then_inc(xs_full, 1)
                if score:
                    turn_qk(3)
                if weigh:
                    values(1)
                if score:
                    v_chunk(1)
                if weigh:
                    turn_p(2)
                    turn_p(3)
                if project:
                    chunk(2)
                if finish:
                    pe.wait_ge(*bank_left(it, "xhT"))
                    nc.tensor.transpose(E[:, 0:S], xh[:, par], ident[:]).then_inc(xhT_full, 1)
                if weigh:
                    values(2)
                if feed:
                    pe.wait_ge(hh_ready, n_(f) + 1)
                    pe.wait_ge(*bank_left(it, "turn_h"))
                    for t in range(KT2):
                        w = min(128, DI - 128 * t)
                        i = nc.tensor.transpose(bank_of("turn_h", 0)[0:w, 128 * t:128 * t + 128], hh[:, 128 * t:128 * t + w],
                                                ident[:])
                    i.then_inc(hT_full, 1)
                if ahead:
                    pe.wait_ge(xw_ready, n_(it + 1) + 1)
                    pe.wait_ge(*bank_left(it, "xT"))
                    nc.tensor.transpose(E[:, 0:S], xw[:, 1 - par], ident[:]).then_inc(xT_full, 1)
                if score:
                    scores(1)
                if project:
                    chunk(3)
                if weigh:
                    turn_o(0)
                    values(3)
                if feed:
                    pe.wait_ge(hT_ready, n_(f) + 1)
                    pe.wait_ge(*bank_left(it, "down"))
                    for t in range(KT2):
                        w = min(128, DI - 128 * t)
                        i = nc.tensor.matmul(E[:, 0:D], hT[0:w, t], weights(f, W2_AT + t * D, D, w), start=(t == 0),
                                             stop=(t == KT2 - 1))
                    i.then_inc(y_full, 1)

            pipeline(pe, step)


def rotary_constants():
    f = np.float32
    half = np.arange(0, DH, 2, dtype=f)
    inv_freq = (f(1.0) / f(10000.0) ** (half / f(DH))).astype(f)
    t = np.arange(S, dtype=f)
    freqs = t[:, None] * inv_freq[None, :]
    base = ((half + f(0.4 * DH)) / f(1.4 * DH)).astype(f)
    power = ((t - S // 2) / f(WINDOW // 2)).astype(f)
    scale = (base[None, :] ** power[:, None]).astype(f)
    cos, sin = np.cos(freqs), np.sin(freqs)
    q = np.stack([np.concatenate([cos * scale * f(8)] * 2, -1), np.concatenate([cos / scale] * 2, -1)], 1)
    s = np.stack([np.concatenate([-sin * scale * f(8), sin * scale * f(8)], -1),
                  np.concatenate([-sin / scale, sin / scale], -1)], 1)
    return q.astype(f), s.astype(f)


def band_mask():
    i, j = np.arange(S)[:, None], np.arange(S)[None, :]
    return np.where((i < j) | (i > j + WINDOW), NEG, 0.0).astype(np.float32)


_INS = ['x', 'ctx_1024', 'L0_ffn_Wqkv', 'L0_ffn_Wo', 'L0_ffn_W1', 'L0_ffn_b1', 'L0_ffn_W2', 'L0_ffn_b2']


def kernel(**inputs):
    import concourse.bacc as _bacc
    from concourse.bass_utils import run_bass_kernel_spmd as _run

    nc = _bacc.Bacc("TRN2", target_bir_lowering=False, num_devices=1)
    arrays, args = {}, []
    cos, sin = rotary_constants()

    def get(name):
        return np.asarray(inputs[name])

    gathered = {
        "by_feature": np.concatenate(
            [get("L0_xattn_Wq").T, get("L0_xattn_Wv").T]
            + [get("L0_xattn_" + v)[:, None] for v in ("bq", "qk_b", "bv")]
            + [get("L0_ffn_ln_g").T, get("L0_ffn_ln_b").T], axis=1),
        "every_token": np.concatenate(
            [get(v).reshape(-1) for v in ("L0_xattn_bv", "g_xattn", "g_ffn", "L0_ffn_q_scale", "L0_ffn_k_scale")]),
        "shape_consts": np.concatenate([cos.reshape(S, -1), sin.reshape(S, -1), band_mask(),
                                        np.eye(128, dtype=np.float32), np.eye(128, k=1, dtype=np.float32)], axis=1)}
    for name in _INS + list(gathered):
        a = gathered[name] if name in gathered else get(name)
        if name == "ctx_1024":
            a = a.swapaxes(-1, -2)
        a = np.ascontiguousarray(a)
        arrays[f"in_{name}_dram"] = a
        args.append(nc.dram_tensor(f"in_{name}_dram", a.shape, mybir.dt.from_np(a.dtype), kind="ExternalInput").ap())
    out = nc.dram_tensor("out_dram", (NB, S, D), mybir.dt.float32, kind="ExternalOutput").ap()
    program(nc, *args, out)
    return _run(nc, [arrays], core_ids=[0]).results[0]["out_dram"]
```
